# Optimizing a Trainium2 kernel written in Bass

```python
import numpy as np
import jax
import jax.numpy as jnp

def _softmax(x, axis=-1):
    return jax.nn.softmax(x, axis=axis)

def _gelu(x):
    return jax.nn.gelu(x, approximate=True)

def _silu(x):
    return jax.nn.silu(x)

def _sigmoid(x):
    return jax.nn.sigmoid(x)

def _layernorm(x, axis=-1, eps=1e-05):
    m = jnp.mean(x, axis=axis, keepdims=True)
    v = jnp.var(x, axis=axis, keepdims=True)
    return (x - m) / jnp.sqrt(v + eps)

def _scatter_add(tgt, idx, src, axis=0):
    return tgt.at[idx].add(src)

def _segment_sum(src, seg, n):
    return jax.ops.segment_sum(src, seg, n)
kernel_name = 'mk_conv_attn_hybrid_d2_conv_nchw512_r4_4f50d7'

def setup_inputs(seed: int=0):
    np.random.seed(seed)
    _w = jnp.asarray

    def _rec_inputs():
        import jax
        import jax.numpy as jnp
        _gk = jax.random.key(seed)
        x = -0.0002928 + 1 * jax.random.normal(jax.random.fold_in(_gk, 1), (2, 128, 16, 16), jnp.float32)
        return x
    x = _rec_inputs()

    def _L0_conv_setup():
        import jax, jax.numpy as jnp
        import numpy as np
        LN_EPS = 1e-05

        def _layernorm_2d(x, w, b):
            mu = jnp.mean(x, axis=(-2, -1), keepdims=True)
            var = jnp.var(x, axis=(-2, -1), keepdims=True)
            return (x - mu) * jax.lax.rsqrt(var + LN_EPS) * w + b
        key = jax.random.key(seed)
        k_x, k_a, k_w, k_b = jax.random.split(key, 4)
        B, T, D = (2, 128, 16)
        x = jax.random.normal(k_x, (B, T, D, D), dtype=jnp.float32)
        log_A = jax.random.normal(k_a, (D,), dtype=jnp.float32) * 0.02
        bound = 1.0 / np.sqrt(D)
        dt_w = jax.random.uniform(k_w, (D,), dtype=jnp.float32, minval=-bound, maxval=bound)
        dt_b = jax.random.uniform(k_b, (1,), dtype=jnp.float32, minval=-bound, maxval=bound)
        ln_w = jnp.ones((D, D), dtype=jnp.float32)
        ln_b = jnp.zeros((D, D), dtype=jnp.float32)
        return {'x': x, 'log_A': log_A, 'dt_w': dt_w, 'dt_b': dt_b, 'ln_w': ln_w, 'ln_b': ln_b}
    _L0_conv_all = _L0_conv_setup()
    _L0_conv_in = {k: v for k, v in _L0_conv_all.items() if k in ('log_A', 'dt_w', 'dt_b', 'ln_w', 'ln_b')}
    del _L0_conv_all

    def _L1_attn_setup():
        import jax, jax.numpy as jnp
        import numpy as np
        B, N, C = (8, 512, 128)

        def _mlp(x, W, b):
            return jax.nn.relu(x @ W + b)
        key = jax.random.key(seed)
        ks = jax.random.split(key, 5)
        s = 1.0 / np.sqrt(C)
        return {'x': jax.random.normal(ks[0], (B, N, C), dtype=jnp.float32), 'Wh': jax.random.normal(ks[1], (C, C), dtype=jnp.float32) * s, 'bh': jnp.zeros((C,), dtype=jnp.float32), 'Wl': jax.random.normal(ks[2], (C, C), dtype=jnp.float32) * s, 'bl': jnp.zeros((C,), dtype=jnp.float32), 'Wg': jax.random.normal(ks[3], (C, C), dtype=jnp.float32) * s, 'bg': jnp.zeros((C,), dtype=jnp.float32), 'Wm': jax.random.normal(ks[4], (C, C), dtype=jnp.float32) * s, 'bm': jnp.zeros((C,), dtype=jnp.float32)}
    _L1_attn_all = _L1_attn_setup()
    _L1_attn_in = {k: v for k, v in _L1_attn_all.items() if k in ('Wh', 'bh', 'Wl', 'bl', 'Wg', 'bg', 'Wm', 'bm')}
    del _L1_attn_all

    def _L1_ffn_setup():
        import jax, jax.numpy as jnp
        import numpy as np
        BINS = jnp.array([-1.5, -1.0, -0.5, 0.0, 0.5, 1.0, 1.5], dtype=jnp.float32)
        N_BINS = BINS.shape[0] + 1
        INDEX = 0
        key = jax.random.key(seed)
        k1, k2 = jax.random.split(key)
        x = jax.random.normal(k1, (8, 1024, 128), dtype=jnp.float32)
        W = jax.random.normal(k2, (N_BINS, 128, 128), dtype=jnp.float32) * 0.02
        return {'x': x, 'W': W}
    _L1_ffn_all = _L1_ffn_setup()
    _L1_ffn_in = {k: v for k, v in _L1_ffn_all.items() if k in ('W',)}
    del _L1_ffn_all
    return {'x': x, 'L0_conv_log_A': _L0_conv_in['log_A'], 'L0_conv_dt_w': _L0_conv_in['dt_w'], 'L0_conv_dt_b': _L0_conv_in['dt_b'], 'L0_conv_ln_w': _L0_conv_in['ln_w'], 'L0_conv_ln_b': _L0_conv_in['ln_b'], 'L1_attn_Wh': _L1_attn_in['Wh'], 'L1_attn_bh': _L1_attn_in['bh'], 'L1_attn_Wl': _L1_attn_in['Wl'], 'L1_attn_bl': _L1_attn_in['bl'], 'L1_attn_Wg': _L1_attn_in['Wg'], 'L1_attn_bg': _L1_attn_in['bg'], 'L1_attn_Wm': _L1_attn_in['Wm'], 'L1_attn_bm': _L1_attn_in['bm'], 'L1_ffn_W': _L1_ffn_in['W']}

def reference(x, L0_conv_log_A, L0_conv_dt_w, L0_conv_dt_b, L0_conv_ln_w, L0_conv_ln_b, L1_attn_Wh, L1_attn_bh, L1_attn_Wl, L1_attn_bl, L1_attn_Wg, L1_attn_bg, L1_attn_Wm, L1_attn_bm, L1_ffn_W):
    import jax
    import jax.numpy as jnp

    def _L0_conv_ref(x, log_A, dt_w, dt_b, ln_w, ln_b):
        import jax, jax.numpy as jnp
        import numpy as np
        LN_EPS = 1e-05

        def _layernorm_2d(x, w, b):
            mu = jnp.mean(x, axis=(-2, -1), keepdims=True)
            var = jnp.var(x, axis=(-2, -1), keepdims=True)
            return (x - mu) * jax.lax.rsqrt(var + LN_EPS) * w + b
        B, T, D, _ = x.shape
        xn = _layernorm_2d(x, ln_w, ln_b)
        A_cont = -jnp.exp(log_A)
        dt = jax.nn.softplus(jnp.einsum('btrc,c->btr', xn, dt_w) + dt_b)
        log_decay = dt * A_cont
        cs = jnp.cumsum(log_decay, axis=1)
        log_M = cs[:, :, None, :] - cs[:, None, :, :]
        idx = jnp.arange(T)
        causal = (idx[:, None] >= idx[None, :])[None, :, :, None]
        M = jnp.exp(jnp.where(causal, log_M, -jnp.inf))
        out = jnp.einsum('btjr,bjrc->btrc', M, xn)
        return out

    def _L1_attn_ref(x, Wh, bh, Wl, bl, Wg, bg, Wm, bm):
        import jax, jax.numpy as jnp
        import numpy as np
        B, N, C = (8, 512, 128)

        def _mlp(x, W, b):
            return jax.nn.relu(x @ W + b)
        h = _mlp(x, Wh, bh)
        l = _mlp(x, Wl, bl)
        scores = jnp.einsum('bnd,bmd->bnm', l, h)
        attn = jax.nn.softmax(scores, axis=-1)
        g = _mlp(x, Wg, bg)
        out = x + jnp.einsum('bnm,bmc->bnc', attn, g)
        return _mlp(out, Wm, bm)

    def _L1_ffn_ref(x, W):
        import jax, jax.numpy as jnp
        import numpy as np
        BINS = jnp.array([-1.5, -1.0, -0.5, 0.0, 0.5, 1.0, 1.5], dtype=jnp.float32)
        N_BINS = BINS.shape[0] + 1
        INDEX = 0
        y = x[..., INDEX]
        mem = jnp.sum(y[..., None] > BINS, axis=-1)
        B, T, D = x.shape
        xf = x.reshape(B * T, D)
        memf = mem.reshape(B * T)
        out = jnp.zeros((B * T, W.shape[-1]), dtype=x.dtype)
        for k in range(N_BINS):
            sel = (memf == k)[:, None].astype(x.dtype)
            out = out + sel * (xf @ W[k])
        return out.reshape(B, T, W.shape[-1])

    def _gn(v, G=32, eps=1e-05):
        B_, C_, H_, W_ = v.shape
        g = v.reshape(B_, G, C_ // G, H_, W_)
        m = jnp.mean(g, axis=(2, 3, 4), keepdims=True)
        s = jnp.var(g, axis=(2, 3, 4), keepdims=True)
        return ((g - m) / jnp.sqrt(s + eps)).reshape(v.shape)

    def _ln_c(v, eps=1e-06):
        m = jnp.mean(v, axis=1, keepdims=True)
        s = jnp.var(v, axis=1, keepdims=True)
        return (v - m) / jnp.sqrt(s + eps)

    def _ln_t(v, eps=1e-05):
        m = jnp.mean(v, axis=-1, keepdims=True)
        s = jnp.var(v, axis=-1, keepdims=True)
        return (v - m) / jnp.sqrt(s + eps)

    def _to_tokens(v):
        B_, C_, H_, W_ = v.shape
        return v.reshape(B_, C_, H_ * W_).transpose(0, 2, 1)

    def _from_tokens(t, like):
        B_, C_, H_, W_ = like.shape
        return t.transpose(0, 2, 1).reshape(B_, C_, H_, W_)
    x = x + _L0_conv_ref(_gn(x), L0_conv_log_A, L0_conv_dt_w, L0_conv_dt_b, L0_conv_ln_w, L0_conv_ln_b)
    t = _to_tokens(x)
    t = t + _L1_attn_ref(_ln_t(t), L1_attn_Wh, L1_attn_bh, L1_attn_Wl, L1_attn_bl, L1_attn_Wg, L1_attn_bg, L1_attn_Wm, L1_attn_bm)
    t = t + _L1_ffn_ref(_ln_t(t), L1_ffn_W)
    x = _from_tokens(t, x)
    return x

_drawn_inputs = setup_inputs


def setup_inputs(seed=0):
    import zlib

    import numpy as np

    out = dict(_drawn_inputs(seed))
    spreads = {'L0_conv_ln_w': (1.0, 0.2),
     'L0_conv_ln_b': (0.0, 0.1),
     'L1_attn_bh': (0.0, 0.291),
     'L1_attn_bl': (0.0, 0.1),
     'L1_attn_bg': (0.0, 0.1),
     'L1_attn_bm': (0.0, 0.1)}
    factors = {'L0_conv_log_A': 5.418}
    for name, (base, spread) in spreads.items():
        noise = np.random.default_rng([zlib.crc32(name.encode()), seed]).standard_normal(out[name].shape)
        drawn = base * np.exp(spread * noise) if base else spread * noise
        out[name] = jnp.asarray(drawn.astype(out[name].dtype))
    for name, factor in factors.items():
        out[name] = (out[name] * factor).astype(out[name].dtype)
    return out
```

```python
from contextlib import ExitStack

import concourse.bass as bass
from concourse import mybir

ALU = mybir.AluOpType
ACT = mybir.ActivationFunctionType
AX_X = mybir.AxisListType.X
F32 = mybir.dt.float32


def conv_attn_hybrid_kernel(
    nc: bass.Bass,
    x: bass.AP,
    log_A: bass.AP,
    dt_w: bass.AP,
    dt_b: bass.AP,
    ln_w: bass.AP,
    ln_b: bass.AP,
    Wh: bass.AP,
    bh: bass.AP,
    Wl: bass.AP,
    bl: bass.AP,
    Wg: bass.AP,
    bg: bass.AP,
    Wm: bass.AP,
    bm: bass.AP,
    W_experts: bass.AP,
    out: bass.AP,
):
    B, C, H, W = x.shape
    P = nc.NUM_PARTITIONS
    N = H * W
    TILES = N // P
    ROWS = P // W
    E = W_experts.shape[0]
    GROUP = C // 32
    BINS = [-1.5, -1.0, -0.5, 0.0, 0.5, 1.0, 1.5]
    EPS = 1e-5
    SOFTPLUS_LINEAR = 40.0
    assert C == P and N % P == 0 and P % W == 0 and E == len(BINS) + 1

    with ExitStack() as ctx:
        def sb(name, shape):
            return ctx.enter_context(nc.sbuf_tensor(name, shape, F32))

        def bank(name):
            return ctx.enter_context(nc.psum_tensor(name, [P, 512], F32))

        def sem(name):
            return ctx.enter_context(nc.semaphore(name))

        identity = sb("identity", [P, P])
        group_mean = sb("group_mean", [P, P])
        row_mask = sb("row_mask", [P, ROWS])
        bins = sb("bins", [P, len(BINS)])
        NVEC = 2 * TILES + 4
        vectors = sb("vectors", [NVEC, P])
        columns = sb("columns", [P, NVEC])
        ln_w_col = [columns[:, j:j + 1] for j in range(TILES)]
        ln_b_col = [columns[:, TILES + j:TILES + j + 1] for j in range(TILES)]
        bh_col, bl_col, bg_col, dt_w_col = [columns[:, 2 * TILES + i:2 * TILES + i + 1] for i in range(4)]
        log_A_row = sb("log_A_row", [P, H])
        A_row = sb("A_row", [P, H])
        dt_b_col = sb("dt_b_col", [P, 1])
        dt_proj = sb("dt_proj", [P, ROWS])
        wh, wl, wg, wm = sb("wh", [P, C]), sb("wl", [P, C]), sb("wg", [P, C]), sb("wm", [P, C])
        bm_row = sb("bm_row", [P, C])
        experts = sb("experts", [P, E, C])

        x_sb = sb("x_sb", [P, B, N])
        partial = sb("partial", [P, B, 6])
        moments = sb("moments", [P, B, 3])
        group_moments = sb("group_moments", [P, B, 2])
        var_eps = sb("var_eps", [P, B])
        mean_sq = sb("mean_sq", [P, B])
        group_var = sb("group_var", [P, B])
        eps_group = sb("eps_group", [P, B])
        row_var = sb("row_var", [P, B])
        row_log = sb("row_log", [P, B])
        row_scale = sb("row_scale", [P, B])
        xhat = sb("xhat", [P, B, N])
        dt_clamped = sb("dt_clamped", [P, B, H])
        dt_exp = sb("dt_exp", [P, B, H])
        dt_log = sb("dt_log", [P, B, H])
        dt_soft = sb("dt_soft", [P, B, H])
        neg_log_decay = sb("neg_log_decay", [P, B, H])
        decay = sb("decay", [P, B, N])
        xn = sb("xn", [P, TILES, B, C])
        scanned = sb("scanned", [P, B, TILES, C])
        tok = sb("tok", [P, B, TILES, C])
        tok_partial = sb("tok_partial", [P, B, TILES, 6])
        tok_moments = sb("tok_moments", [P, B, TILES, 2])
        tok_log = sb("tok_log", [P, B, TILES])
        tok_scale = sb("tok_scale", [P, B, TILES])
        u = sb("u", [P, B, TILES, C])
        uT = sb("uT", [P, B, N])
        hT, lT, gT = sb("hT", [P, B, N]), sb("lT", [P, B, N]), sb("gT", [P, B, N])
        neg_max = sb("neg_max", [P, B, TILES])
        prob_sum = sb("prob_sum", [P, B, TILES])
        prob_scale = sb("prob_scale", [P, B, TILES])
        probs = sb("probs", [P, B, TILES, N])
        probsT = sb("probsT", [P, B, TILES, TILES, P])
        values = sb("values", [P, B, TILES, C])
        skip = sb("skip", [P, B, TILES, C])
        mixed = sb("mixed", [P, B, TILES, C])
        tok2 = sb("tok2", [P, B, TILES, C])
        tok2_partial = sb("tok2_partial", [P, B, TILES, 6])
        tok2_moments = sb("tok2_moments", [P, B, TILES, 2])
        tok2_log = sb("tok2_log", [P, B, TILES])
        tok2_scale = sb("tok2_scale", [P, B, TILES])
        v = sb("v", [P, B, TILES, C])
        bin_hits = sb("bin_hits", [P, B, TILES, len(BINS)])
        bin_index = sb("bin_index", [P, B, TILES])
        vT = sb("vT", [P, B, N])
        v_picked = sb("v_picked", [P, B, E, N])
        out_sb = sb("out_sb", [P, B, N])

        banks = [bank(f"bank{i}") for i in range(8)]
        columns_ps = banks[7][:, 0:NVEC]
        group_ps = banks[0][:, 0:2 * B].rearrange("p (b s) -> p b s", s=2)
        xhatT_ps = [banks[1 + j][:, 0:B * C].rearrange("p (b c) -> p b c", b=B) for j in range(TILES)]
        dt_ps = banks[6][:, 0:B * H].rearrange("p (b h) -> p b h", b=B)
        decayT_ps = [banks[3 + b][:, 0:TILES * C].rearrange("p (j c) -> p j c", j=TILES) for b in range(B)]
        xT_ps = banks[5][:, :].rearrange("p (b j c) -> p b j c", b=B, j=TILES)

        def token_tiles(b, n):
            return banks[4 * b + n][:, 0:N].rearrange("p (i c) -> p i c", i=TILES)

        uT_ps = [banks[4 * b][:, 0:N] for b in range(B)]
        hT_ps = [banks[4 * b + 1][:, 0:N] for b in range(B)]
        lT_ps = [banks[4 * b + 2][:, 0:N] for b in range(B)]
        gT_ps = [banks[4 * b + 3][:, 0:N] for b in range(B)]
        scores_ps = [[banks[4 * b + i][:, 0:N] for i in range(TILES)] for b in range(B)]
        skip_ps = [token_tiles(b, 2) for b in range(B)]
        values_ps = [token_tiles(b, 3) for b in range(B)]
        probsT_ps = [[token_tiles(b, 2 + i) for i in range(TILES)] for b in range(B)]
        attended_ps = [[banks[4 * b + i][:, 0:C] for i in range(TILES)] for b in range(B)]
        vT_ps = [banks[4 * b][:, 0:N] for b in range(B)]
        bin_ps = [banks[4 * b + 1][:, 0:N] for b in range(B)]
        out_ps = [banks[4 * b + 2][:, 0:N] for b in range(B)]

        x_loaded = [sem(f"x_loaded{b}") for b in range(B)]
        vectors_loaded = sem("vectors_loaded")
        decay_params_loaded = sem("decay_params_loaded")
        wh_loaded, wl_loaded, wg_loaded, wm_loaded = sem("wh_loaded"), sem("wl_loaded"), sem("wg_loaded"), sem("wm_loaded")
        bm_loaded = sem("bm_loaded")
        experts_loaded = sem("experts_loaded")
        out_stored = sem("out_stored")
        pool_filled = sem("pool_filled")
        identity_ready = sem("identity_ready")
        group_half_cut = sem("group_half_cut")
        group_mean_ready = sem("group_mean_ready")
        mask_half_cut = sem("mask_half_cut")
        row_mask_ready = sem("row_mask_ready")
        bins_ready = sem("bins_ready")
        columns_turned = sem("columns_turned")
        xT_ready = sem("xT_ready")
        group_summed = sem("group_summed")
        xhatT_ready = sem("xhatT_ready")
        dt_projected = sem("dt_projected")
        decayT_ready = sem("decayT_ready")
        uT_turned = sem("uT_turned")
        h_projected = sem("h_projected")
        l_projected = sem("l_projected")
        g_projected = sem("g_projected")
        scores_ready = sem("scores_ready")
        skip_projected = sem("skip_projected")
        values_projected = sem("values_projected")
        probs_turned = sem("probs_turned")
        attended = sem("attended")
        v_turned = sem("v_turned")
        bins_spread = sem("bins_spread")
        experts_done = sem("experts_done")
        columns_ready = sem("columns_ready")
        dt_proj_ready = sem("dt_proj_ready")
        partial_ready = sem("partial_ready")
        mean_var_ready = sem("mean_var_ready")
        moments_ready = sem("moments_ready")
        var_eps_ready = sem("var_eps_ready")
        group_copied = sem("group_copied")
        mean_sq_ready = sem("mean_sq_ready")
        group_var_ready = sem("group_var_ready")
        eps_group_ready = sem("eps_group_ready")
        row_var_ready = sem("row_var_ready")
        xhat_ready = sem("xhat_ready")
        xn_ready = [sem(f"xn_ready{j}") for j in range(TILES)]
        dt_clamped_ready = sem("dt_clamped_ready")
        dt_soft_ready = sem("dt_soft_ready")
        neg_log_decay_ready = sem("neg_log_decay_ready")
        scan_ready = sem("scan_ready")
        tok_ready = sem("tok_ready")
        tok_partial_ready = sem("tok_partial_ready")
        tok_moments_ready = sem("tok_moments_ready")
        u_ready = sem("u_ready")
        lT_ready = sem("lT_ready")
        neg_max_ready = sem("neg_max_ready")
        prob_scale_ready = sem("prob_scale_ready")
        skip_ready = sem("skip_ready")
        mixed_ready = sem("mixed_ready")
        tok2_ready = sem("tok2_ready")
        tok2_partial_ready = sem("tok2_partial_ready")
        tok2_moments_ready = sem("tok2_moments_ready")
        v_ready = sem("v_ready")
        bin_index_ready = sem("bin_index_ready")
        picked_ready = sem("picked_ready")
        A_ready = sem("A_ready")
        row_log_ready = sem("row_log_ready")
        row_scale_ready = sem("row_scale_ready")
        dt_exp_ready = sem("dt_exp_ready")
        dt_log_ready = sem("dt_log_ready")
        decay_ready = sem("decay_ready")
        tok_log_ready = sem("tok_log_ready")
        tok_scale_ready = sem("tok_scale_ready")
        uT_ready = sem("uT_ready")
        hT_ready = sem("hT_ready")
        gT_ready = sem("gT_ready")
        probs_ready = sem("probs_ready")
        values_ready = sem("values_ready")
        probsT_ready = [sem(f"probsT_ready{i}") for i in range(TILES)]
        tok2_log_ready = sem("tok2_log_ready")
        tok2_scale_ready = sem("tok2_scale_ready")
        vT_ready = sem("vT_ready")
        out_ready = sem("out_ready")

        x_dram = x.rearrange("b c h w -> b c (h w)")
        out_dram = out.rearrange("b c h w -> b c (h w)")
        ln_w_dram = ln_w.rearrange("(j r) c -> j (r c)", j=TILES)
        ln_b_dram = ln_b.rearrange("(j r) c -> j (r c)", j=TILES)

        def as_row(a):
            return a.rearrange("(o n) -> o n", o=1)

        block = ctx.enter_context(nc.Block())

        @block.sync
        def _(sp):
            for b in range(B):
                sp.dma_start(x_sb[:, b, :], x_dram[b]).then_inc(x_loaded[b], 16)
            sp.dma_start(wh[:, :], Wh).then_inc(wh_loaded, 16)
            sp.dma_start(wl[:, :], Wl).then_inc(wl_loaded, 16)
            sp.dma_start(wg[:, :], Wg).then_inc(wg_loaded, 16)
            sp.dma_start(wm[:, :], Wm).then_inc(wm_loaded, 16)
            sp.dma_start(bm_row[:, :], as_row(bm).partition_broadcast(P)).then_inc(bm_loaded, 16)
            sp.dma_start(experts[:, :, :], W_experts.rearrange("e i o -> i e o")).then_inc(experts_loaded, 16)
            for b in range(B):
                sp.wait_ge(out_ready, b + 1)
                sp.dma_start(out_dram[b], out_sb[:, b, :]).then_inc(out_stored, 16)
            sp.wait_ge(out_stored, 16 * B)

        @block.gpsimd
        def _(pool):
            nc.gpsimd.memset(identity[:, :], 0.0).then_inc(pool_filled, 1)
            nc.gpsimd.memset(group_mean[:, :], 1.0 / GROUP).then_inc(pool_filled, 1)
            nc.gpsimd.memset(row_mask[:, :], 1.0).then_inc(pool_filled, 1)
            pool.wait_ge(pool_filled, 3)
            nc.gpsimd.affine_select(out=identity[:, :], in_=identity[:, :], compare_op=ALU.not_equal, fill=1.0,
                                    base=0, pattern=[[-1, P]], channel_multiplier=1).then_inc(identity_ready, 1)
            grouped = group_mean[:, :].rearrange("p (g k) -> p g k", k=GROUP)
            nc.gpsimd.affine_select(out=grouped, in_=grouped, compare_op=ALU.is_ge, fill=0.0, base=0,
                                    pattern=[[-GROUP, P // GROUP], [0, GROUP]],
                                    channel_multiplier=1).then_inc(group_half_cut, 1)
            pool.wait_ge(group_half_cut, 1)
            nc.gpsimd.affine_select(out=grouped, in_=grouped, compare_op=ALU.is_ge, fill=0.0, base=GROUP - 1,
                                    pattern=[[GROUP, P // GROUP], [0, GROUP]],
                                    channel_multiplier=-1).then_inc(group_mean_ready, 1)
            nc.gpsimd.affine_select(out=row_mask[:, :], in_=row_mask[:, :], compare_op=ALU.is_ge, fill=0.0, base=0,
                                    pattern=[[-W, ROWS]], channel_multiplier=1).then_inc(mask_half_cut, 1)
            pool.wait_ge(mask_half_cut, 1)
            nc.gpsimd.affine_select(out=row_mask[:, :], in_=row_mask[:, :], compare_op=ALU.is_ge, fill=0.0,
                                    base=W - 1, pattern=[[W, ROWS]],
                                    channel_multiplier=-1).then_inc(row_mask_ready, 1)
            for i, edge in enumerate(BINS):
                nc.gpsimd.memset(bins[:, i:i + 1], edge).then_inc(bins_ready, 1)

        @block.tensor
        def _(pe):
            def turn_x(b):
                pe.wait_ge(x_loaded[b], 16)
                for j in range(TILES):
                    nc.tensor.transpose(xT_ps[:, b, j, :], x_sb[:, b, j * P:(j + 1) * P],
                                        identity[:, :]).then_inc(xT_ready, 1)

            def project_tokens(b):
                pe.wait_ge(uT_ready, b + 1)
                if b == 0:
                    pe.wait_ge(wh_loaded, 16)
                nc.tensor.matmul(hT_ps[b], wh[:, :], uT[:, b, :], start=True, stop=True).then_inc(h_projected, 1)
                if b == 0:
                    pe.wait_ge(wl_loaded, 16)
                nc.tensor.matmul(lT_ps[b], wl[:, :], uT[:, b, :], start=True, stop=True).then_inc(l_projected, 1)
                if b == 0:
                    pe.wait_ge(wg_loaded, 16)
                nc.tensor.matmul(gT_ps[b], wg[:, :], uT[:, b, :], start=True, stop=True).then_inc(g_projected, 1)

            def turn_tokens(b):
                for i in range(TILES):
                    pe.wait_ge(u_ready, TILES * b + i + 1)
                    last = nc.tensor.transpose(uT_ps[b][:, i * P:(i + 1) * P], u[:, b, i, :], identity[:, :])
                last.then_inc(uT_turned, 1)

            def score(b):
                pe.wait_ge(hT_ready, b + 1)
                pe.wait_ge(lT_ready, b + 1)
                for i in range(TILES):
                    nc.tensor.matmul(scores_ps[b][i], lT[:, b, i * P:(i + 1) * P], hT[:, b, :],
                                     start=True, stop=True).then_inc(scores_ready, 1)

            def project_skip_and_values(b):
                if b == 0:
                    pe.wait_ge(wm_loaded, 16)
                for i in range(TILES):
                    last = nc.tensor.matmul(skip_ps[b][:, i, :], uT[:, b, i * P:(i + 1) * P], wm[:, :],
                                            start=True, stop=True)
                last.then_inc(skip_projected, 1)
                pe.wait_ge(gT_ready, b + 1)
                for i in range(TILES):
                    last = nc.tensor.matmul(values_ps[b][:, i, :], gT[:, b, i * P:(i + 1) * P], wm[:, :],
                                            start=True, stop=True)
                last.then_inc(values_projected, 1)

            def turn_probs(b, i):
                pe.wait_ge(probs_ready, TILES * b + i + 1)
                if i == 0:
                    pe.wait_ge(skip_ready, b + 1)
                else:
                    pe.wait_ge(values_ready, b + 1)
                for m in range(TILES):
                    last = nc.tensor.transpose(probsT_ps[b][i][:, m, :], probs[:, b, i, m * P:(m + 1) * P],
                                               identity[:, :])
                last.then_inc(probs_turned, 1)

            def attend(b, i):
                pe.wait_ge(values_ready, b + 1)
                pe.wait_ge(probsT_ready[i], b + 1)
                for m in range(TILES):
                    last = nc.tensor.matmul(attended_ps[b][i], probsT[:, b, i, m, :], values[:, b, m, :],
                                            start=(m == 0), stop=(m == TILES - 1))
                last.then_inc(attended, 1)

            def carry_residual(b):
                for i in range(TILES):
                    pe.wait_ge(tok2_ready, TILES * b + i + 1)
                    nc.tensor.matmul(out_ps[b][:, i * P:(i + 1) * P], tok2[:, b, i, :], identity[:, :],
                                     start=(i == 0), stop=False, skip_group_check=True)

            def turn_v(b):
                for i in range(TILES):
                    pe.wait_ge(v_ready, TILES * b + i + 1)
                    last = nc.tensor.transpose(vT_ps[b][:, i * P:(i + 1) * P], v[:, b, i, :], identity[:, :])
                last.then_inc(v_turned, 1)
                for i in range(TILES):
                    pe.wait_ge(bin_index_ready, TILES * b + i + 1)
                    last = nc.tensor.transpose(bin_ps[b][:, i * P:(i + 1) * P],
                                               bin_index[:, b, i:i + 1].to_broadcast([P, P]), identity[:, :])
                last.then_inc(bins_spread, 1)

            def run_experts(b):
                if b == 0:
                    pe.wait_ge(experts_loaded, 16)
                for e in range(E):
                    pe.wait_ge(picked_ready, E * b + e + 1)
                    last = nc.tensor.matmul(out_ps[b], experts[:, e, :], v_picked[:, b, e, :],
                                            start=False, stop=(e == E - 1), skip_group_check=True)
                last.then_inc(experts_done, 1)

            pe.wait_ge(identity_ready, 1)
            pe.wait_ge(vectors_loaded, 16 * 6)
            nc.tensor.transpose(columns_ps, vectors[:, :], identity[0:NVEC, 0:NVEC]).then_inc(columns_turned, 1)
            for b in range(B):
                turn_x(b)
            pe.wait_ge(group_mean_ready, 1)
            pe.wait_ge(moments_ready, B)
            nc.tensor.matmul(group_ps, group_mean[:, :], moments[:, :, 0:3:2], start=True,
                             stop=True).then_inc(group_summed, 1)
            for b in range(B):
                pe.wait_ge(xhat_ready, b + 1)
                for j in range(TILES):
                    nc.tensor.transpose(xhatT_ps[j][:, b, :], xhat[:, b, j * P:(j + 1) * P],
                                        identity[:, :]).then_inc(xhatT_ready, 1)
            pe.wait_ge(dt_proj_ready, 1)
            for j in range(TILES):
                pe.wait_ge(xn_ready[j], 1)
                for b in range(B):
                    last = nc.tensor.matmul(dt_ps[:, b, j * ROWS:(j + 1) * ROWS], xn[:, j, b, :], dt_proj[:, :],
                                            start=True, stop=True)
            last.then_inc(dt_projected, 1)
            for b in range(B):
                pe.wait_ge(decay_ready, b + 1)
                for j in range(TILES):
                    last = nc.tensor.transpose(decayT_ps[b][:, j, :], decay[:, b, j * P:(j + 1) * P], identity[:, :])
                last.then_inc(decayT_ready, 1)
            for b in range(B):
                turn_tokens(b)
                project_tokens(b)
                score(b)
                project_skip_and_values(b)
            for b in range(B):
                for i in range(TILES):
                    turn_probs(b, i)
                for i in range(TILES):
                    attend(b, i)
            for b in range(B):
                pe.wait_ge(probsT_ready[0], b + 1)
                carry_residual(b)
                turn_v(b)
                run_experts(b)

        @block.vector
        def _(dve):
            def token_moments(b, i):
                dve.wait_ge(tok_ready, b + 1)
                nc.vector.bn_stats(tok_partial[:, b, i, :], tok[:, b, i, :]).then_inc(tok_partial_ready, 1)
                dve.wait_ge(tok_partial_ready, TILES * b + i + 1)
                nc.vector.bn_aggr(tok_moments[:, b, i, :], tok_partial[:, b, i, :]).then_inc(tok_moments_ready, 1)

            def scan_and_add(b):
                dve.wait_ge(decayT_ready, b + 1)
                for j in range(TILES):
                    dve.wait_ge(xn_ready[j], 1)
                    nc.vector.tensor_tensor_scan(scanned[:, b, j, :], decayT_ps[b][:, j, :], xn[:, j, b, :], 0.0,
                                                 ALU.mult, ALU.add).then_inc(scan_ready, 1)
                dve.wait_ge(scan_ready, TILES * (b + 1))
                dve.wait_ge(xT_ready, TILES * (b + 1))
                nc.vector.tensor_tensor(tok[:, b, :, :], scanned[:, b, :, :], xT_ps[:, b, :, :],
                                        ALU.add).then_inc(tok_ready, 1)
                for i in range(TILES):
                    token_moments(b, i)

            def normalize_tokens(b):
                dve.wait_ge(tok_scale_ready, b + 1)
                for i in range(TILES):
                    nc.vector.tensor_scalar(u[:, b, i, :], tok[:, b, i, :], tok_moments[:, b, i, 0:1],
                                            tok_scale[:, b, i:i + 1], ALU.subtract, ALU.mult).then_inc(u_ready, 1)

            def relu_l(b):
                dve.wait_ge(l_projected, b + 1)
                nc.vector.tensor_scalar(lT[:, b, :], lT_ps[b], bl_col, 0.0, ALU.add, ALU.max).then_inc(lT_ready, 1)

            def score_max(b):
                for i in range(TILES):
                    dve.wait_ge(scores_ready, TILES * b + i + 1)
                    nc.vector.tensor_reduce(neg_max[:, b, i:i + 1], scores_ps[b][i], AX_X, ALU.max,
                                            negate=True).then_inc(neg_max_ready, 1)

            def add_skip_bias(b):
                dve.wait_ge(skip_projected, b + 1)
                if b == 0:
                    dve.wait_ge(bm_loaded, 16)
                nc.vector.tensor_tensor(skip[:, b, :, :], skip_ps[b],
                                        bm_row[:, :].unsqueeze(1).to_broadcast([P, TILES, C]),
                                        ALU.add).then_inc(skip_ready, 1)

            def scale_probs(b, i):
                dve.wait_ge(probs_ready, TILES * b + i + 1)
                nc.vector.reciprocal(prob_scale[:, b, i:i + 1], prob_sum[:, b, i:i + 1]).then_inc(prob_scale_ready, 1)

            def copy_probsT(b, i):
                dve.wait_ge(probs_turned, TILES * b + i + 1)
                nc.vector.tensor_copy(probsT[:, b, i, :, :], probsT_ps[b][i]).then_inc(probsT_ready[i], 1)

            def mix(b, i):
                n = TILES * b + i + 1
                dve.wait_ge(attended, n)
                dve.wait_ge(skip_ready, b + 1)
                dve.wait_ge(prob_scale_ready, n)
                nc.vector.scalar_tensor_tensor(mixed[:, b, i, :], attended_ps[b][i], prob_scale[:, b, i:i + 1],
                                               skip[:, b, i, :], ALU.mult, ALU.add).then_inc(mixed_ready, 1)
                dve.wait_ge(mixed_ready, n)
                nc.vector.scalar_tensor_tensor(tok2[:, b, i, :], mixed[:, b, i, :], 0.0, tok[:, b, i, :],
                                               ALU.max, ALU.add).then_inc(tok2_ready, 1)
                dve.wait_ge(tok2_ready, n)
                nc.vector.bn_stats(tok2_partial[:, b, i, :], tok2[:, b, i, :]).then_inc(tok2_partial_ready, 1)
                dve.wait_ge(tok2_partial_ready, n)
                nc.vector.bn_aggr(tok2_moments[:, b, i, :], tok2_partial[:, b, i, :]).then_inc(tok2_moments_ready, 1)

            def normalize_tokens2(b):
                dve.wait_ge(tok2_scale_ready, b + 1)
                for i in range(TILES):
                    nc.vector.tensor_scalar(v[:, b, i, :], tok2[:, b, i, :], tok2_moments[:, b, i, 0:1],
                                            tok2_scale[:, b, i:i + 1], ALU.subtract, ALU.mult).then_inc(v_ready, 1)
                if b == 0:
                    dve.wait_ge(bins_ready, len(BINS))
                for i in range(TILES):
                    dve.wait_ge(v_ready, TILES * b + i + 1)
                    nc.vector.tensor_scalar(bin_hits[:, b, i, :], bins[:, :], v[:, b, i, 0:1], None, ALU.is_lt,
                                            ALU.add, accum_out=bin_index[:, b, i:i + 1]).then_inc(bin_index_ready, 1)

            def pick(b):
                dve.wait_ge(bins_spread, b + 1)
                dve.wait_ge(vT_ready, b + 1)
                for e in range(E):
                    nc.vector.scalar_tensor_tensor(v_picked[:, b, e, :], bin_ps[b], float(e), vT[:, b, :],
                                                   ALU.is_equal, ALU.mult).then_inc(picked_ready, 1)

            for b in range(B):
                dve.wait_ge(x_loaded[b], 16)
                nc.vector.bn_stats(partial[:, b, :], x_sb[:, b, :]).then_inc(partial_ready, 1)
            for b in range(B):
                dve.wait_ge(partial_ready, b + 1)
                nc.vector.bn_aggr(moments[:, b, 0:2], partial[:, b, :]).then_inc(mean_var_ready, 1)
            for b in range(B):
                dve.wait_ge(mean_var_ready, b + 1)
                nc.vector.scalar_tensor_tensor(moments[:, b, 2:3], moments[:, b, 0:1], moments[:, b, 0:1],
                                               moments[:, b, 1:2], ALU.mult, ALU.add).then_inc(moments_ready, 1)
            nc.vector.tensor_scalar(var_eps[:, :], moments[:, :, 1], EPS * EPS, None, ALU.add).then_inc(var_eps_ready, 1)
            dve.wait_ge(columns_turned, 1)
            nc.vector.tensor_copy(columns[:, :], columns_ps).then_inc(columns_ready, 1)
            dve.wait_ge(columns_ready, 1)
            dve.wait_ge(row_mask_ready, 1)
            nc.vector.tensor_scalar(dt_proj[:, :], row_mask[:, :], dt_w_col, None, ALU.mult).then_inc(dt_proj_ready, 1)
            dve.wait_ge(group_summed, 1)
            nc.vector.tensor_copy(group_moments[:, :, :], group_ps).then_inc(group_copied, 1)
            dve.wait_ge(group_copied, 1)
            nc.vector.tensor_tensor(mean_sq[:, :], group_moments[:, :, 0], group_moments[:, :, 0],
                                    ALU.mult).then_inc(mean_sq_ready, 1)
            dve.wait_ge(mean_sq_ready, 1)
            nc.vector.tensor_tensor(group_var[:, :], group_moments[:, :, 1], mean_sq[:, :],
                                    ALU.subtract).then_inc(group_var_ready, 1)
            dve.wait_ge(group_var_ready, 1)
            nc.vector.tensor_scalar(eps_group[:, :], group_var[:, :], 0.0, EPS, ALU.max,
                                    ALU.mult).then_inc(eps_group_ready, 1)
            dve.wait_ge(eps_group_ready, 1)
            dve.wait_ge(var_eps_ready, 1)
            nc.vector.tensor_tensor(row_var[:, :], eps_group[:, :], var_eps[:, :], ALU.add).then_inc(row_var_ready, 1)
            dve.wait_ge(row_scale_ready, 1)
            for b in range(B):
                nc.vector.tensor_scalar(xhat[:, b, :], x_sb[:, b, :], moments[:, b, 0:1], row_scale[:, b:b + 1],
                                        ALU.subtract, ALU.mult).then_inc(xhat_ready, 1)
            dve.wait_ge(xhatT_ready, TILES * (B - 1) + 1)
            nc.vector.tensor_scalar(xn[:, 0, :, :], xhatT_ps[0], ln_w_col[0], ln_b_col[0], ALU.mult,
                                    ALU.add).then_inc(xn_ready[0], 1)
            dve.wait_ge(dt_projected, 1)
            dve.wait_ge(decay_params_loaded, 32)
            nc.vector.tensor_scalar(dt_clamped[:, :, :], dt_ps, dt_b_col[:, 0:1], SOFTPLUS_LINEAR, ALU.add,
                                    ALU.min).then_inc(dt_clamped_ready, 1)
            dve.wait_ge(dt_log_ready, 1)
            nc.vector.scalar_tensor_tensor(dt_soft[:, :, :], dt_ps, dt_b_col[:, 0:1], dt_log[:, :, :], ALU.add,
                                           ALU.max).then_inc(dt_soft_ready, 1)
            dve.wait_ge(dt_soft_ready, 1)
            dve.wait_ge(A_ready, 1)
            nc.vector.tensor_tensor(neg_log_decay[:, :, :], dt_soft[:, :, :],
                                    A_row[:, :].unsqueeze(1).to_broadcast([P, B, H]),
                                    ALU.mult).then_inc(neg_log_decay_ready, 1)
            for b in range(B):
                scan_and_add(b)
                normalize_tokens(b)
            for b in range(B):
                relu_l(b)
                score_max(b)
                add_skip_bias(b)
            for b in range(B):
                for i in range(TILES):
                    scale_probs(b, i)
                copy_probsT(b, 1)
                for i in range(TILES):
                    mix(b, i)
            for b in range(B):
                normalize_tokens2(b)
                pick(b)

        @block.scalar
        def _(act):
            act.dma_start(vectors[0:TILES, :], ln_w_dram).then_inc(vectors_loaded, 16)
            act.dma_start(vectors[TILES:2 * TILES, :], ln_b_dram).then_inc(vectors_loaded, 16)
            for i, bias in enumerate((bh, bl, bg)):
                act.dma_start(vectors[2 * TILES + i:2 * TILES + i + 1, :], as_row(bias)).then_inc(vectors_loaded, 16)
            act.dma_start(vectors[NVEC - 1:NVEC, :].rearrange("p (r c) -> p r c", c=W),
                          as_row(dt_w).unsqueeze(1).to_broadcast([1, ROWS, W])).then_inc(vectors_loaded, 16)
            act.dma_start(log_A_row[:, :], as_row(log_A).partition_broadcast(P)).then_inc(decay_params_loaded, 16)
            act.dma_start(dt_b_col[:, :], as_row(dt_b).partition_broadcast(P)).then_inc(decay_params_loaded, 16)

            def token_scale(b):
                act.wait_ge(tok_moments_ready, TILES * (b + 1))
                nc.scalar.activation(tok_log[:, b, :], tok_moments[:, b, :, 1], ACT.Ln,
                                     bias=EPS).then_inc(tok_log_ready, 1)
                act.wait_ge(tok_log_ready, b + 1)
                nc.scalar.activation(tok_scale[:, b, :], tok_log[:, b, :], ACT.Exp, scale=-0.5).then_inc(tok_scale_ready, 1)

            def copy_uT(b):
                act.wait_ge(uT_turned, b + 1)
                nc.scalar.copy(uT[:, b, :], uT_ps[b]).then_inc(uT_ready, 1)

            def relu_h(b):
                act.wait_ge(h_projected, b + 1)
                nc.scalar.activation(hT[:, b, :], hT_ps[b], ACT.Relu, bias=bh_col).then_inc(hT_ready, 1)

            def relu_g(b):
                act.wait_ge(g_projected, b + 1)
                nc.scalar.activation(gT[:, b, :], gT_ps[b], ACT.Relu, bias=bg_col).then_inc(gT_ready, 1)

            def exponentiate(b, i):
                act.wait_ge(neg_max_ready, TILES * b + i + 1)
                nc.scalar.activation(probs[:, b, i, :], scores_ps[b][i], ACT.Exp, bias=neg_max[:, b, i:i + 1],
                                     accum_out=prob_sum[:, b, i:i + 1]).then_inc(probs_ready, 1)

            def copy_values(b):
                act.wait_ge(values_projected, b + 1)
                nc.scalar.copy(values[:, b, :, :], values_ps[b]).then_inc(values_ready, 1)

            def copy_probsT(b, i):
                act.wait_ge(probs_turned, TILES * b + i + 1)
                nc.scalar.copy(probsT[:, b, i, :, :], probsT_ps[b][i]).then_inc(probsT_ready[i], 1)

            def token_scale2(b):
                act.wait_ge(tok2_moments_ready, TILES * (b + 1))
                nc.scalar.activation(tok2_log[:, b, :], tok2_moments[:, b, :, 1], ACT.Ln,
                                     bias=EPS).then_inc(tok2_log_ready, 1)
                act.wait_ge(tok2_log_ready, b + 1)
                nc.scalar.activation(tok2_scale[:, b, :], tok2_log[:, b, :], ACT.Exp,
                                     scale=-0.5).then_inc(tok2_scale_ready, 1)

            def copy_vT(b):
                act.wait_ge(v_turned, b + 1)
                nc.scalar.copy(vT[:, b, :], vT_ps[b]).then_inc(vT_ready, 1)

            def copy_out(b):
                act.wait_ge(experts_done, b + 1)
                nc.scalar.copy(out_sb[:, b, :], out_ps[b]).then_inc(out_ready, 1)

            act.wait_ge(decay_params_loaded, 32)
            nc.scalar.activation(A_row[:, :], log_A_row[:, :], ACT.Exp).then_inc(A_ready, 1)
            act.wait_ge(row_var_ready, 1)
            nc.scalar.activation(row_log[:, :], row_var[:, :], ACT.Ln).then_inc(row_log_ready, 1)
            act.wait_ge(row_log_ready, 1)
            nc.scalar.activation(row_scale[:, :], row_log[:, :], ACT.Exp, scale=-0.5).then_inc(row_scale_ready, 1)
            act.wait_ge(columns_ready, 1)
            act.wait_ge(xhatT_ready, TILES * B)
            nc.scalar.activation(xn[:, 1, :, :], xhatT_ps[1], ACT.Identity, bias=ln_b_col[1],
                                 scale=ln_w_col[1]).then_inc(xn_ready[1], 1)
            act.wait_ge(dt_clamped_ready, 1)
            nc.scalar.activation(dt_exp[:, :, :], dt_clamped[:, :, :], ACT.Exp).then_inc(dt_exp_ready, 1)
            act.wait_ge(dt_exp_ready, 1)
            nc.scalar.activation(dt_log[:, :, :], dt_exp[:, :, :], ACT.Ln, bias=1.0).then_inc(dt_log_ready, 1)
            act.wait_ge(neg_log_decay_ready, 1)
            for b in range(B):
                nc.scalar.activation(decay[:, b, :].rearrange("p (h w) -> p h w", w=W),
                                     neg_log_decay[:, b, :].unsqueeze(2).to_broadcast([P, H, W]), ACT.Exp,
                                     scale=-1.0).then_inc(decay_ready, 1)
            for b in range(B):
                token_scale(b)
                copy_uT(b)
                relu_h(b)
                relu_g(b)
            for b in range(B):
                exponentiate(b, 0)
                exponentiate(b, 1)
                copy_values(b)
                copy_probsT(b, 0)
            for b in range(B):
                token_scale2(b)
                copy_vT(b)
            for b in range(B):
                copy_out(b)


_INS = ['x', 'L0_conv_log_A', 'L0_conv_dt_w', 'L0_conv_dt_b', 'L0_conv_ln_w', 'L0_conv_ln_b', 'L1_attn_Wh',
        'L1_attn_bh', 'L1_attn_Wl', 'L1_attn_bl', 'L1_attn_Wg', 'L1_attn_bg', 'L1_attn_Wm', 'L1_attn_bm', 'L1_ffn_W']
_OUTS = [((2, 128, 16, 16), 'float32')]


def kernel(**inputs):
    import numpy as _np
    import concourse.bacc as _bacc
    from concourse import mybir as _mybir
    from concourse.bass_utils import run_bass_kernel_spmd as _run

    nc = _bacc.Bacc("TRN2", target_bir_lowering=False, num_devices=1)
    arrays, args = {}, []
    for name in _INS:
        a = _np.ascontiguousarray(inputs[name])
        arrays[f"in_{name}_dram"] = a
        args.append(nc.dram_tensor(f"in_{name}_dram", a.shape, _mybir.dt.from_np(a.dtype), kind="ExternalInput").ap())
    for i, (shape, dtype) in enumerate(_OUTS):
        dt = _mybir.dt.from_np(_np.dtype(dtype))
        args.append(nc.dram_tensor(f"out_{i}_dram", shape, dt, kind="ExternalOutput").ap())
    conv_attn_hybrid_kernel(nc, *args)
    r = _run(nc, [arrays], core_ids=[0])
    got = tuple(r.results[0][f"out_{i}_dram"] for i in range(len(_OUTS)))
    return got[0]
```

```python
from contextlib import ExitStack

import concourse.bass as bass
from concourse import mybir

ALU = mybir.AluOpType
ACT = mybir.ActivationFunctionType
AX_X = mybir.AxisListType.X
F32 = mybir.dt.float32


def conv_attn_hybrid_kernel(
    nc: bass.Bass,
    x: bass.AP,
    small_params: bass.AP,
    attn_weights: bass.AP,
    W_experts: bass.AP,
    out: bass.AP,
):
    B, C, H, W = x.shape
    P = nc.NUM_PARTITIONS
    N = H * W
    TILES = N // P
    ROWS = P // W
    E = W_experts.shape[1]
    GROUP = C // 32
    BINS = [-1.5, -1.0, -0.5, 0.0, 0.5, 1.0, 1.5]
    EPS = 1e-5
    SOFTPLUS_LINEAR = 40.0
    assert C == P and N % P == 0 and P % W == 0 and E == len(BINS) + 1

    with ExitStack() as ctx:
        def sb(name, shape):
            return ctx.enter_context(nc.sbuf_tensor(name, shape, F32))

        def bank(name):
            return ctx.enter_context(nc.psum_tensor(name, [P, 512], F32))

        def sem(name):
            return ctx.enter_context(nc.semaphore(name))

        turn = sb("turn", [P, P + ROWS])
        identity = turn[:, 0:P]
        row_mask = turn[:, P:P + ROWS]
        group_mean = sb("group_mean", [P, P])
        bins = sb("bins", [P, len(BINS)])
        params = sb("params", [P, 2 * TILES + 5 + H + C])
        ln_col = params[:, 0:2 * TILES]
        bh_col, bl_col, bg_col, dt_w_col, dt_b_col = [params[:, 2 * TILES + i:2 * TILES + i + 1] for i in range(5)]
        log_A_row = params[:, 2 * TILES + 5:2 * TILES + 5 + H]
        bm_row = params[:, 2 * TILES + 5 + H:2 * TILES + 5 + H + C]
        ln_w_col = [ln_col[:, j:j + 1] for j in range(TILES)]
        ln_b_col = [ln_col[:, TILES + j:TILES + j + 1] for j in range(TILES)]
        ln_dt = sb("ln_dt", [P, 2 * TILES])
        A_row = sb("A_row", [P, H])
        attn_w = sb("attn_w", [P, 4, C])
        wh, wl, wg, wm = [attn_w[:, i, :] for i in range(4)]
        experts = sb("experts", [P, E, C])

        x_sb = sb("x_sb", [P, B, N])
        partial = sb("partial", [P, B, 6])
        moments = sb("moments", [P, B, 3])
        group_moments = sb("group_moments", [P, B, 2])
        var_eps = sb("var_eps", [P, B])
        mean_sq = sb("mean_sq", [P, B])
        group_var = sb("group_var", [P, B])
        eps_group = sb("eps_group", [P, B])
        row_var = sb("row_var", [P, B])
        row_log = sb("row_log", [P, B])
        row_scale = sb("row_scale", [P, B])
        xhat = sb("xhat", [P, B, N])
        x_proj = sb("x_proj", [P, B, N])
        x_row = sb("x_row", [P, B, H])
        x_centred = sb("x_centred", [P, B, H])
        dt_bias = sb("dt_bias", [P, H])
        dt = sb("dt", [P, B, H])
        dt_clamped = sb("dt_clamped", [P, B, H])
        dt_exp = sb("dt_exp", [P, B, H])
        dt_log = sb("dt_log", [P, B, H])
        dt_soft = sb("dt_soft", [P, B, H])
        neg_log_decay = sb("neg_log_decay", [P, B, H])
        decay = sb("decay", [P, B, N])
        xn = sb("xn", [P, B, TILES, C])
        scanned = sb("scanned", [P, B, TILES, C])
        tok = sb("tok", [P, B, TILES, C])
        tok_partial = sb("tok_partial", [P, B, TILES, 6])
        tok_moments = sb("tok_moments", [P, B, TILES, 2])
        tok_log = sb("tok_log", [P, B, TILES])
        tok_scale = sb("tok_scale", [P, B, TILES])
        u = sb("u", [P, B, TILES, C])
        uT = sb("uT", [P, B, N])
        hT, lT, gT = sb("hT", [P, B, N]), sb("lT", [P, B, N]), sb("gT", [P, B, N])
        neg_max = sb("neg_max", [P, B, TILES])
        prob_sum = sb("prob_sum", [P, B, TILES])
        prob_scale = sb("prob_scale", [P, B, TILES])
        probs = sb("probs", [P, B, TILES, N])
        probsT = sb("probsT", [P, B, TILES, TILES, P])
        values = sb("values", [P, B, TILES, C])
        skip = sb("skip", [P, B, TILES, C])
        mixed = sb("mixed", [P, B, TILES, C])
        tok2 = sb("tok2", [P, B, TILES, C])
        tok2_partial = sb("tok2_partial", [P, B, TILES, 6])
        tok2_moments = sb("tok2_moments", [P, B, TILES, 2])
        tok2_log = sb("tok2_log", [P, B, TILES])
        tok2_scale = sb("tok2_scale", [P, B, TILES])
        v = sb("v", [P, B, TILES, C])
        bin_hits = sb("bin_hits", [P, B, TILES, len(BINS)])
        bin_index = sb("bin_index", [P, B, TILES])
        vT = sb("vT", [P, B, N])
        v_picked = sb("v_picked", [P, B, E, N])
        out_sb = sb("out_sb", [P, B, N])

        banks = [bank(f"bank{i}") for i in range(8)]
        group_ps = banks[0][:, 0:2 * B].rearrange("p (b s) -> p b s", s=2)
        ln_dt_ps = banks[6][:, 0:TILES * (P + ROWS)].rearrange("p (j k) -> p j k", j=TILES)
        dt_bias_ps = banks[6][:, TILES * (P + ROWS):TILES * (P + ROWS) + H]
        xhatT_ps = [[banks[(1, 2, 0, 7)[TILES * b + j]][:, 0:C] for j in range(TILES)] for b in range(B)]
        decayT_ps = [banks[3 + b][:, 0:TILES * C].rearrange("p (j c) -> p j c", j=TILES) for b in range(B)]
        xT_ps = banks[5][:, :].rearrange("p (b j c) -> p b j c", b=B, j=TILES)

        def token_tiles(b, n):
            return banks[4 * b + n][:, 0:N].rearrange("p (i c) -> p i c", i=TILES)

        uT_ps = [banks[4 * b][:, 0:N] for b in range(B)]
        hT_ps = [banks[4 * b + 1][:, 0:N] for b in range(B)]
        lT_ps = [banks[4 * b + 2][:, 0:N] for b in range(B)]
        gT_ps = [banks[4 * b + 3][:, 0:N] for b in range(B)]
        scores_ps = [[banks[4 * b + i][:, 0:N] for i in range(TILES)] for b in range(B)]
        skip_ps = [token_tiles(b, 2) for b in range(B)]
        values_ps = [token_tiles(b, 3) for b in range(B)]
        probsT_ps = [[token_tiles(b, 2 + i) for i in range(TILES)] for b in range(B)]
        attended_ps = [[banks[4 * b + i][:, 0:C] for i in range(TILES)] for b in range(B)]
        vT_ps = [banks[4 * b][:, 0:N] for b in range(B)]
        bin_ps = [banks[4 * b + 1][:, 0:N] for b in range(B)]
        out_ps = [banks[4 * b + 2][:, 0:N] for b in range(B)]

        x_loaded = [sem(f"x_loaded{b}") for b in range(B)]
        params_loaded = sem("params_loaded")
        attn_w_loaded = sem("attn_w_loaded")
        experts_loaded = sem("experts_loaded")
        out_stored = sem("out_stored")
        pool_filled = sem("pool_filled")
        identity_ready = sem("identity_ready")
        group_half_cut = sem("group_half_cut")
        group_mean_ready = sem("group_mean_ready")
        mask_half_cut = sem("mask_half_cut")
        row_mask_ready = sem("row_mask_ready")
        bins_ready = sem("bins_ready")
        ln_dt_ready = sem("ln_dt_ready")
        ln_dt_spread = sem("ln_dt_spread")
        xT_ready = sem("xT_ready")
        group_summed = sem("group_summed")
        xhatT_ready = sem("xhatT_ready")
        decayT_ready = sem("decayT_ready")
        uT_turned = sem("uT_turned")
        h_projected = sem("h_projected")
        l_projected = sem("l_projected")
        g_projected = sem("g_projected")
        scores_ready = sem("scores_ready")
        skip_projected = sem("skip_projected")
        values_projected = sem("values_projected")
        probs_turned = sem("probs_turned")
        attended = sem("attended")
        v_turned = sem("v_turned")
        bins_spread = sem("bins_spread")
        experts_done = sem("experts_done")
        x_proj_ready = sem("x_proj_ready")
        x_row_ready = sem("x_row_ready")
        x_centred_ready = sem("x_centred_ready")
        dt_bias_ready = sem("dt_bias_ready")
        dt_ready = sem("dt_ready")
        partial_ready = sem("partial_ready")
        mean_var_ready = sem("mean_var_ready")
        moments_ready = sem("moments_ready")
        var_eps_ready = sem("var_eps_ready")
        group_copied = sem("group_copied")
        mean_sq_ready = sem("mean_sq_ready")
        group_var_ready = sem("group_var_ready")
        eps_group_ready = sem("eps_group_ready")
        row_var_ready = sem("row_var_ready")
        xhat_ready = sem("xhat_ready")
        xn_ready = [sem(f"xn_ready{j}") for j in range(TILES)]
        dt_clamped_ready = sem("dt_clamped_ready")
        dt_soft_ready = sem("dt_soft_ready")
        neg_log_decay_ready = sem("neg_log_decay_ready")
        scan_ready = sem("scan_ready")
        tok_ready = sem("tok_ready")
        tok_partial_ready = sem("tok_partial_ready")
        tok_moments_ready = sem("tok_moments_ready")
        u_ready = sem("u_ready")
        gT_ready = sem("gT_ready")
        neg_max_ready = sem("neg_max_ready")
        prob_scale_ready = sem("prob_scale_ready")
        skip_ready = sem("skip_ready")
        mixed_ready = sem("mixed_ready")
        tok2_ready = sem("tok2_ready")
        tok2_partial_ready = sem("tok2_partial_ready")
        tok2_moments_ready = sem("tok2_moments_ready")
        v_ready = sem("v_ready")
        bin_index_ready = sem("bin_index_ready")
        picked_ready = sem("picked_ready")
        A_ready = sem("A_ready")
        row_log_ready = sem("row_log_ready")
        row_scale_ready = sem("row_scale_ready")
        dt_exp_ready = sem("dt_exp_ready")
        dt_log_ready = sem("dt_log_ready")
        decay_ready = sem("decay_ready")
        tok_log_ready = sem("tok_log_ready")
        tok_scale_ready = sem("tok_scale_ready")
        uT_ready = sem("uT_ready")
        hT_ready = sem("hT_ready")
        lT_ready = sem("lT_ready")
        probs_ready = sem("probs_ready")
        values_ready = sem("values_ready")
        probsT_ready = [sem(f"probsT_ready{i}") for i in range(TILES)]
        tok2_log_ready = sem("tok2_log_ready")
        tok2_scale_ready = sem("tok2_scale_ready")
        vT_ready = sem("vT_ready")
        out_ready = sem("out_ready")

        x_dram = x.rearrange("b c h w -> b c (h w)")
        out_dram = out.rearrange("b c h w -> b c (h w)")

        block = ctx.enter_context(nc.Block())

        @block.sync
        def _(sp):
            for b in range(B):
                sp.dma_start(x_sb[:, b, :], x_dram[b]).then_inc(x_loaded[b], 16)
            sp.dma_start(params[:, :], small_params).then_inc(params_loaded, 16)
            sp.dma_start(attn_w[:, :, :], attn_weights).then_inc(attn_w_loaded, 16)
            sp.dma_start(experts[:, :, :], W_experts).then_inc(experts_loaded, 16)
            for b in range(B):
                sp.wait_ge(out_ready, b + 1)
                sp.dma_start(out_dram[b], out_sb[:, b, :]).then_inc(out_stored, 16)
            sp.wait_ge(out_stored, 16 * B)

        @block.gpsimd
        def _(pool):
            nc.gpsimd.memset(identity, 0.0).then_inc(pool_filled, 1)
            nc.gpsimd.memset(group_mean[:, :], 1.0 / GROUP).then_inc(pool_filled, 1)
            nc.gpsimd.memset(row_mask, 1.0).then_inc(pool_filled, 1)
            pool.wait_ge(pool_filled, 3)
            nc.gpsimd.affine_select(out=identity, in_=identity, compare_op=ALU.not_equal, fill=1.0,
                                    base=0, pattern=[[-1, P]], channel_multiplier=1).then_inc(identity_ready, 1)
            grouped = group_mean[:, :].rearrange("p (g k) -> p g k", k=GROUP)
            nc.gpsimd.affine_select(out=grouped, in_=grouped, compare_op=ALU.is_ge, fill=0.0, base=0,
                                    pattern=[[-GROUP, P // GROUP], [0, GROUP]],
                                    channel_multiplier=1).then_inc(group_half_cut, 1)
            pool.wait_ge(group_half_cut, 1)
            nc.gpsimd.affine_select(out=grouped, in_=grouped, compare_op=ALU.is_ge, fill=0.0, base=GROUP - 1,
                                    pattern=[[GROUP, P // GROUP], [0, GROUP]],
                                    channel_multiplier=-1).then_inc(group_mean_ready, 1)
            nc.gpsimd.affine_select(out=row_mask, in_=row_mask, compare_op=ALU.is_ge, fill=0.0, base=0,
                                    pattern=[[-W, ROWS]], channel_multiplier=1).then_inc(mask_half_cut, 1)
            pool.wait_ge(mask_half_cut, 1)
            nc.gpsimd.affine_select(out=row_mask, in_=row_mask, compare_op=ALU.is_ge, fill=0.0,
                                    base=W - 1, pattern=[[W, ROWS]],
                                    channel_multiplier=-1).then_inc(row_mask_ready, 1)
            for i, edge in enumerate(BINS):
                nc.gpsimd.memset(bins[:, i:i + 1], edge).then_inc(bins_ready, 1)
            pool.wait_ge(params_loaded, 16)
            nc.gpsimd.tensor_scalar(ln_dt[:, :], ln_col, dt_w_col, None, ALU.mult).then_inc(ln_dt_ready, 1)

        @block.tensor
        def _(pe):
            def turn_x(b):
                pe.wait_ge(x_loaded[b], 16)
                for j in range(TILES):
                    nc.tensor.transpose(xT_ps[:, b, j, :], x_sb[:, b, j * P:(j + 1) * P],
                                        identity).then_inc(xT_ready, 1)

            def project_tokens(b):
                pe.wait_ge(uT_ready, b + 1)
                if b == 0:
                    pe.wait_ge(attn_w_loaded, 16)
                nc.tensor.matmul(hT_ps[b], wh, uT[:, b, :], start=True, stop=True).then_inc(h_projected, 1)
                nc.tensor.matmul(lT_ps[b], wl, uT[:, b, :], start=True, stop=True).then_inc(l_projected, 1)
                nc.tensor.matmul(gT_ps[b], wg, uT[:, b, :], start=True, stop=True).then_inc(g_projected, 1)

            def turn_tokens(b):
                for i in range(TILES):
                    pe.wait_ge(u_ready, TILES * b + i + 1)
                    last = nc.tensor.transpose(uT_ps[b][:, i * P:(i + 1) * P], u[:, b, i, :], identity)
                last.then_inc(uT_turned, 1)

            def score(b):
                pe.wait_ge(hT_ready, b + 1)
                pe.wait_ge(lT_ready, b + 1)
                for i in range(TILES):
                    nc.tensor.matmul(scores_ps[b][i], lT[:, b, i * P:(i + 1) * P], hT[:, b, :],
                                     start=True, stop=True).then_inc(scores_ready, 1)

            def project_skip_and_values(b):
                for i in range(TILES):
                    last = nc.tensor.matmul(skip_ps[b][:, i, :], uT[:, b, i * P:(i + 1) * P], wm,
                                            start=True, stop=True)
                last.then_inc(skip_projected, 1)
                pe.wait_ge(gT_ready, b + 1)
                for i in range(TILES):
                    last = nc.tensor.matmul(values_ps[b][:, i, :], gT[:, b, i * P:(i + 1) * P], wm,
                                            start=True, stop=True)
                last.then_inc(values_projected, 1)

            def turn_probs(b, i):
                pe.wait_ge(probs_ready, TILES * b + i + 1)
                if i == 0:
                    pe.wait_ge(skip_ready, b + 1)
                else:
                    pe.wait_ge(values_ready, b + 1)
                for m in range(TILES):
                    last = nc.tensor.transpose(probsT_ps[b][i][:, m, :], probs[:, b, i, m * P:(m + 1) * P],
                                               identity)
                last.then_inc(probs_turned, 1)

            def attend(b, i):
                pe.wait_ge(values_ready, b + 1)
                pe.wait_ge(probsT_ready[i], b + 1)
                for m in range(TILES):
                    last = nc.tensor.matmul(attended_ps[b][i], probsT[:, b, i, m, :], values[:, b, m, :],
                                            start=(m == 0), stop=(m == TILES - 1))
                last.then_inc(attended, 1)

            def carry_residual(b):
                pe.wait_ge(probsT_ready[0], b + 1)
                for i in range(TILES):
                    pe.wait_ge(tok2_ready, TILES * b + i + 1)
                    nc.tensor.matmul(out_ps[b][:, i * P:(i + 1) * P], tok2[:, b, i, :], identity,
                                     start=(i == 0), stop=False, skip_group_check=True)

            def turn_v(b):
                for i in range(TILES):
                    pe.wait_ge(v_ready, TILES * b + i + 1)
                    last = nc.tensor.transpose(vT_ps[b][:, i * P:(i + 1) * P], v[:, b, i, :], identity)
                last.then_inc(v_turned, 1)
                for i in range(TILES):
                    pe.wait_ge(bin_index_ready, TILES * b + i + 1)
                    last = nc.tensor.transpose(bin_ps[b][:, i * P:(i + 1) * P],
                                               bin_index[:, b, i:i + 1].to_broadcast([P, P]), identity)
                last.then_inc(bins_spread, 1)

            def run_experts(b, first, end):
                if b == 0 and first == 0:
                    pe.wait_ge(experts_loaded, 16)
                for e in range(first, end):
                    pe.wait_ge(picked_ready, E * b + e + 1)
                    last = nc.tensor.matmul(out_ps[b], experts[:, e, :], v_picked[:, b, e, :],
                                            start=False, stop=(e == E - 1), skip_group_check=True)
                if end == E:
                    last.then_inc(experts_done, 1)

            pe.wait_ge(identity_ready, 1)
            for b in range(B):
                turn_x(b)
            pe.wait_ge(row_mask_ready, 1)
            pe.wait_ge(ln_dt_ready, 1)
            for j in range(TILES):
                nc.tensor.matmul(ln_dt_ps[:, j, :], ln_dt[:, j:j + 1].to_broadcast([P, P]), turn[:, :],
                                 start=True, stop=True)
            for j in range(TILES):
                last = nc.tensor.matmul(dt_bias_ps[:, j * ROWS:(j + 1) * ROWS],
                                        ln_dt[:, TILES + j:TILES + j + 1].to_broadcast([P, P]), row_mask,
                                        start=True, stop=True)
            last.then_inc(ln_dt_spread, 1)
            pe.wait_ge(group_mean_ready, 1)
            pe.wait_ge(moments_ready, B)
            nc.tensor.matmul(group_ps, group_mean[:, :], moments[:, :, 0:3:2], start=True,
                             stop=True).then_inc(group_summed, 1)
            for b in range(B):
                pe.wait_ge(xhat_ready, b + 1)
                if b == 1:
                    pe.wait_ge(group_copied, 1)
                for j in range(TILES):
                    nc.tensor.transpose(xhatT_ps[b][j], xhat[:, b, j * P:(j + 1) * P],
                                        identity).then_inc(xhatT_ready, 1)
            for b in range(B):
                pe.wait_ge(decay_ready, b + 1)
                for j in range(TILES):
                    last = nc.tensor.transpose(decayT_ps[b][:, j, :], decay[:, b, j * P:(j + 1) * P], identity)
                last.then_inc(decayT_ready, 1)
            turn_tokens(0)
            project_tokens(0)
            score(0)
            turn_tokens(1)
            project_skip_and_values(0)
            project_tokens(1)
            turn_probs(0, 0)
            turn_probs(0, 1)
            score(1)
            attend(0, 0)
            attend(0, 1)
            project_skip_and_values(1)
            turn_probs(1, 0)
            turn_probs(1, 1)
            carry_residual(0)
            attend(1, 0)
            attend(1, 1)
            turn_v(0)
            run_experts(0, 0, 4)
            carry_residual(1)
            run_experts(0, 4, 6)
            turn_v(1)
            run_experts(0, 6, E)
            run_experts(1, 0, E)

        @block.vector
        def _(dve):
            def scan_and_add(b):
                dve.wait_ge(decayT_ready, b + 1)
                for j in range(TILES):
                    dve.wait_ge(xn_ready[j], b + 1)
                    nc.vector.tensor_tensor_scan(scanned[:, b, j, :], decayT_ps[b][:, j, :], xn[:, b, j, :], 0.0,
                                                 ALU.mult, ALU.add).then_inc(scan_ready, 1)
                dve.wait_ge(scan_ready, TILES * (b + 1))
                dve.wait_ge(xT_ready, TILES * (b + 1))
                nc.vector.tensor_tensor(tok[:, b, :, :], scanned[:, b, :, :], xT_ps[:, b, :, :],
                                        ALU.add).then_inc(tok_ready, 1)
                dve.wait_ge(tok_ready, b + 1)
                for i in range(TILES):
                    nc.vector.bn_stats(tok_partial[:, b, i, :], tok[:, b, i, :]).then_inc(tok_partial_ready, 1)
                for i in range(TILES):
                    dve.wait_ge(tok_partial_ready, TILES * b + i + 1)
                    nc.vector.bn_aggr(tok_moments[:, b, i, :], tok_partial[:, b, i, :]).then_inc(tok_moments_ready, 1)

            def normalize_tokens(b):
                dve.wait_ge(tok_scale_ready, b + 1)
                for i in range(TILES):
                    nc.vector.tensor_scalar(u[:, b, i, :], tok[:, b, i, :], tok_moments[:, b, i, 0:1],
                                            tok_scale[:, b, i:i + 1], ALU.subtract, ALU.mult).then_inc(u_ready, 1)

            def relu_g(b):
                dve.wait_ge(g_projected, b + 1)
                nc.vector.tensor_scalar(gT[:, b, :], gT_ps[b], bg_col, 0.0, ALU.add, ALU.max).then_inc(gT_ready, 1)

            def score_max(b):
                for i in range(TILES):
                    dve.wait_ge(scores_ready, TILES * b + i + 1)
                    nc.vector.tensor_reduce(neg_max[:, b, i:i + 1], scores_ps[b][i], AX_X, ALU.max,
                                            negate=True).then_inc(neg_max_ready, 1)

            def add_skip_bias(b):
                dve.wait_ge(skip_projected, b + 1)
                nc.vector.tensor_tensor(skip[:, b, :, :], skip_ps[b],
                                        bm_row.unsqueeze(1).to_broadcast([P, TILES, C]),
                                        ALU.add).then_inc(skip_ready, 1)

            def scale_probs(b, i):
                dve.wait_ge(probs_ready, TILES * b + i + 1)
                nc.vector.reciprocal(prob_scale[:, b, i:i + 1], prob_sum[:, b, i:i + 1]).then_inc(prob_scale_ready, 1)

            def copy_probsT(b, i):
                dve.wait_ge(probs_turned, TILES * b + i + 1)
                nc.vector.tensor_copy(probsT[:, b, i, :, :], probsT_ps[b][i]).then_inc(probsT_ready[i], 1)

            def mix(b):
                dve.wait_ge(skip_ready, b + 1)
                for i in range(TILES):
                    n = TILES * b + i + 1
                    dve.wait_ge(attended, n)
                    dve.wait_ge(prob_scale_ready, n)
                    nc.vector.scalar_tensor_tensor(mixed[:, b, i, :], attended_ps[b][i], prob_scale[:, b, i:i + 1],
                                                   skip[:, b, i, :], ALU.mult, ALU.add).then_inc(mixed_ready, 1)
                for i in range(TILES):
                    dve.wait_ge(mixed_ready, TILES * b + i + 1)
                    nc.vector.scalar_tensor_tensor(tok2[:, b, i, :], mixed[:, b, i, :], 0.0, tok[:, b, i, :],
                                                   ALU.max, ALU.add).then_inc(tok2_ready, 1)
                for i in range(TILES):
                    dve.wait_ge(tok2_ready, TILES * b + i + 1)
                    nc.vector.bn_stats(tok2_partial[:, b, i, :], tok2[:, b, i, :]).then_inc(tok2_partial_ready, 1)
                for i in range(TILES):
                    dve.wait_ge(tok2_partial_ready, TILES * b + i + 1)
                    nc.vector.bn_aggr(tok2_moments[:, b, i, :],
                                      tok2_partial[:, b, i, :]).then_inc(tok2_moments_ready, 1)

            def normalize_tokens2(b):
                dve.wait_ge(tok2_scale_ready, b + 1)
                for i in range(TILES):
                    nc.vector.tensor_scalar(v[:, b, i, :], tok2[:, b, i, :], tok2_moments[:, b, i, 0:1],
                                            tok2_scale[:, b, i:i + 1], ALU.subtract, ALU.mult).then_inc(v_ready, 1)
                if b == 0:
                    dve.wait_ge(bins_ready, len(BINS))
                for i in range(TILES):
                    dve.wait_ge(v_ready, TILES * b + i + 1)
                    nc.vector.tensor_scalar(bin_hits[:, b, i, :], bins[:, :], v[:, b, i, 0:1], None, ALU.is_lt,
                                            ALU.add, accum_out=bin_index[:, b, i:i + 1]).then_inc(bin_index_ready, 1)

            def pick(b, first, end):
                dve.wait_ge(bins_spread, b + 1)
                dve.wait_ge(vT_ready, b + 1)
                for e in range(first, end):
                    nc.vector.scalar_tensor_tensor(v_picked[:, b, e, :], bin_ps[b], float(e), vT[:, b, :],
                                                   ALU.is_equal, ALU.mult).then_inc(picked_ready, 1)

            for b in range(B):
                dve.wait_ge(x_loaded[b], 16)
                nc.vector.bn_stats(partial[:, b, :], x_sb[:, b, :]).then_inc(partial_ready, 1)
            for b in range(B):
                dve.wait_ge(partial_ready, b + 1)
                nc.vector.bn_aggr(moments[:, b, 0:2], partial[:, b, :]).then_inc(mean_var_ready, 1)
            for b in range(B):
                dve.wait_ge(mean_var_ready, b + 1)
                nc.vector.scalar_tensor_tensor(moments[:, b, 2:3], moments[:, b, 0:1], moments[:, b, 0:1],
                                               moments[:, b, 1:2], ALU.mult, ALU.add).then_inc(moments_ready, 1)
            nc.vector.tensor_scalar(var_eps[:, :], moments[:, :, 1], EPS * EPS, None, ALU.add).then_inc(var_eps_ready, 1)
            dve.wait_ge(ln_dt_spread, 1)
            for b in range(B):
                nc.vector.tensor_tensor(x_proj[:, b, :].rearrange("p (j n) -> p j n", j=TILES),
                                        x_sb[:, b, :].rearrange("p (j n) -> p j n", j=TILES),
                                        ln_dt_ps[:, :, 0:P], ALU.mult).then_inc(x_proj_ready, 1)
            dve.wait_ge(group_summed, 1)
            nc.vector.tensor_copy(group_moments[:, :, :], group_ps).then_inc(group_copied, 1)
            dve.wait_ge(group_copied, 1)
            nc.vector.tensor_tensor(mean_sq[:, :], group_moments[:, :, 0], group_moments[:, :, 0],
                                    ALU.mult).then_inc(mean_sq_ready, 1)
            dve.wait_ge(mean_sq_ready, 1)
            nc.vector.tensor_tensor(group_var[:, :], group_moments[:, :, 1], mean_sq[:, :],
                                    ALU.subtract).then_inc(group_var_ready, 1)
            dve.wait_ge(group_var_ready, 1)
            nc.vector.tensor_scalar(eps_group[:, :], group_var[:, :], 0.0, EPS, ALU.max,
                                    ALU.mult).then_inc(eps_group_ready, 1)
            dve.wait_ge(eps_group_ready, 1)
            dve.wait_ge(var_eps_ready, 1)
            nc.vector.tensor_tensor(row_var[:, :], eps_group[:, :], var_eps[:, :], ALU.add).then_inc(row_var_ready, 1)
            dve.wait_ge(x_proj_ready, B)
            nc.vector.tensor_reduce(x_row[:, :, :], x_proj[:, :, :].rearrange("p b (h w) -> p b h w", w=W), AX_X,
                                    ALU.add).then_inc(x_row_ready, 1)
            nc.vector.tensor_scalar(dt_bias[:, :], dt_bias_ps, dt_b_col, None, ALU.add).then_inc(dt_bias_ready, 1)
            dve.wait_ge(x_row_ready, 1)
            for b in range(B):
                nc.vector.scalar_tensor_tensor(x_centred[:, b, :].rearrange("p (j r) -> p j r", j=TILES),
                                               ln_dt_ps[:, :, P:P + ROWS], moments[:, b, 0:1],
                                               x_row[:, b, :].rearrange("p (j r) -> p j r", j=TILES), ALU.mult,
                                               ALU.subtract, reverse1=True).then_inc(x_centred_ready, 1)
            dve.wait_ge(row_scale_ready, 1)
            dve.wait_ge(dt_bias_ready, 1)
            for b in range(B):
                dve.wait_ge(x_centred_ready, b + 1)
                nc.vector.scalar_tensor_tensor(dt[:, b, :], x_centred[:, b, :], row_scale[:, b:b + 1], dt_bias[:, :],
                                               ALU.mult, ALU.add).then_inc(dt_ready, 1)
            dve.wait_ge(dt_ready, B)
            nc.vector.tensor_scalar(dt_clamped[:, :, :], dt[:, :, :], SOFTPLUS_LINEAR, None,
                                    ALU.min).then_inc(dt_clamped_ready, 1)
            for b in range(B):
                nc.vector.tensor_scalar(xhat[:, b, :], x_sb[:, b, :], moments[:, b, 0:1], row_scale[:, b:b + 1],
                                        ALU.subtract, ALU.mult).then_inc(xhat_ready, 1)
            dve.wait_ge(dt_log_ready, 1)
            nc.vector.tensor_tensor(dt_soft[:, :, :], dt[:, :, :], dt_log[:, :, :], ALU.max).then_inc(dt_soft_ready, 1)
            dve.wait_ge(dt_soft_ready, 1)
            dve.wait_ge(A_ready, 1)
            nc.vector.tensor_tensor(neg_log_decay[:, :, :], dt_soft[:, :, :],
                                    A_row[:, :].unsqueeze(1).to_broadcast([P, B, H]),
                                    ALU.mult).then_inc(neg_log_decay_ready, 1)
            for b in range(B):
                dve.wait_ge(xhatT_ready, TILES * b + 1)
                nc.vector.tensor_scalar(xn[:, b, 0, :], xhatT_ps[b][0], ln_w_col[0], ln_b_col[0], ALU.mult,
                                        ALU.add).then_inc(xn_ready[0], 1)
            scan_and_add(0)
            normalize_tokens(0)
            scan_and_add(1)
            relu_g(0)
            normalize_tokens(1)
            score_max(0)
            add_skip_bias(0)
            relu_g(1)
            score_max(1)
            copy_probsT(0, 1)
            for i in range(TILES):
                scale_probs(0, i)
            mix(0)
            add_skip_bias(1)
            copy_probsT(1, 1)
            for i in range(TILES):
                scale_probs(1, i)
            normalize_tokens2(0)
            pick(0, 0, 2)
            mix(1)
            pick(0, 2, 5)
            normalize_tokens2(1)
            pick(0, 5, E)
            pick(1, 0, E)

        @block.scalar
        def _(act):
            nc.scalar.preload_act_table_set("natural_log_exp_and_others")
            def token_scale(b):
                act.wait_ge(tok_moments_ready, TILES * (b + 1))
                nc.scalar.activation(tok_log[:, b, :], tok_moments[:, b, :, 1], ACT.Ln,
                                     bias=EPS).then_inc(tok_log_ready, 1)
                act.wait_ge(tok_log_ready, b + 1)
                nc.scalar.activation(tok_scale[:, b, :], tok_log[:, b, :], ACT.Exp, scale=-0.5).then_inc(tok_scale_ready, 1)

            def copy_uT(b):
                act.wait_ge(uT_turned, b + 1)
                nc.scalar.copy(uT[:, b, :], uT_ps[b]).then_inc(uT_ready, 1)

            def relu_h(b):
                act.wait_ge(h_projected, b + 1)
                nc.scalar.activation(hT[:, b, :], hT_ps[b], ACT.Relu, bias=bh_col).then_inc(hT_ready, 1)

            def relu_l(b):
                act.wait_ge(l_projected, b + 1)
                nc.scalar.activation(lT[:, b, :], lT_ps[b], ACT.Relu, bias=bl_col).then_inc(lT_ready, 1)

            def exponentiate(b, i):
                act.wait_ge(neg_max_ready, TILES * b + i + 1)
                nc.scalar.activation(probs[:, b, i, :], scores_ps[b][i], ACT.Exp, bias=neg_max[:, b, i:i + 1],
                                     accum_out=prob_sum[:, b, i:i + 1]).then_inc(probs_ready, 1)

            def copy_values(b):
                act.wait_ge(values_projected, b + 1)
                nc.scalar.copy(values[:, b, :, :], values_ps[b]).then_inc(values_ready, 1)

            def copy_probsT(b, i):
                act.wait_ge(probs_turned, TILES * b + i + 1)
                nc.scalar.copy(probsT[:, b, i, :, :], probsT_ps[b][i]).then_inc(probsT_ready[i], 1)

            def token_scale2(b):
                act.wait_ge(tok2_moments_ready, TILES * (b + 1))
                nc.scalar.activation(tok2_log[:, b, :], tok2_moments[:, b, :, 1], ACT.Ln,
                                     bias=EPS).then_inc(tok2_log_ready, 1)
                act.wait_ge(tok2_log_ready, b + 1)
                nc.scalar.activation(tok2_scale[:, b, :], tok2_log[:, b, :], ACT.Exp,
                                     scale=-0.5).then_inc(tok2_scale_ready, 1)

            def copy_vT(b):
                act.wait_ge(v_turned, b + 1)
                nc.scalar.copy(vT[:, b, :], vT_ps[b]).then_inc(vT_ready, 1)

            def copy_out(b):
                act.wait_ge(experts_done, b + 1)
                nc.scalar.copy(out_sb[:, b, :], out_ps[b]).then_inc(out_ready, 1)

            act.wait_ge(params_loaded, 16)
            nc.scalar.activation(A_row[:, :], log_A_row, ACT.Exp).then_inc(A_ready, 1)
            act.wait_ge(row_var_ready, 1)
            nc.scalar.activation(row_log[:, :], row_var[:, :], ACT.Ln).then_inc(row_log_ready, 1)
            act.wait_ge(row_log_ready, 1)
            nc.scalar.activation(row_scale[:, :], row_log[:, :], ACT.Exp, scale=-0.5).then_inc(row_scale_ready, 1)
            act.wait_ge(dt_clamped_ready, 1)
            nc.scalar.activation(dt_exp[:, :, :], dt_clamped[:, :, :], ACT.Exp).then_inc(dt_exp_ready, 1)
            act.wait_ge(dt_exp_ready, 1)
            nc.scalar.activation(dt_log[:, :, :], dt_exp[:, :, :], ACT.Ln, bias=1.0).then_inc(dt_log_ready, 1)
            for b in range(B):
                act.wait_ge(xhatT_ready, TILES * b + 2)
                nc.scalar.activation(xn[:, b, 1, :], xhatT_ps[b][1], ACT.Identity, bias=ln_b_col[1],
                                     scale=ln_w_col[1]).then_inc(xn_ready[1], 1)
            act.wait_ge(neg_log_decay_ready, 1)
            for b in range(B):
                nc.scalar.activation(decay[:, b, :].rearrange("p (h w) -> p h w", w=W),
                                     neg_log_decay[:, b, :].unsqueeze(2).to_broadcast([P, H, W]), ACT.Exp,
                                     scale=-1.0).then_inc(decay_ready, 1)
            token_scale(0)
            copy_uT(0)
            relu_h(0)
            relu_l(0)
            token_scale(1)
            copy_uT(1)
            exponentiate(0, 0)
            exponentiate(0, 1)
            copy_values(0)
            relu_h(1)
            relu_l(1)
            copy_probsT(0, 0)
            exponentiate(1, 0)
            exponentiate(1, 1)
            token_scale2(0)
            copy_values(1)
            copy_probsT(1, 0)
            copy_vT(0)
            token_scale2(1)
            copy_vT(1)
            copy_out(0)
            copy_out(1)


_OUTS = [((2, 128, 16, 16), 'float32')]


def kernel(x, L0_conv_log_A, L0_conv_dt_w, L0_conv_dt_b, L0_conv_ln_w, L0_conv_ln_b, L1_attn_Wh, L1_attn_bh,
           L1_attn_Wl, L1_attn_bl, L1_attn_Wg, L1_attn_bg, L1_attn_Wm, L1_attn_bm, L1_ffn_W):
    import numpy as _np
    import concourse.bacc as _bacc
    from concourse import mybir as _mybir
    from concourse.bass_utils import run_bass_kernel_spmd as _run

    P, W = 128, x.shape[3]
    columns = [_np.asarray(a).reshape(-1, P).T for a in (L0_conv_ln_w, L0_conv_ln_b, L1_attn_bh, L1_attn_bl, L1_attn_bg)]
    columns.append(_np.tile(_np.asarray(L0_conv_dt_w), P // W).reshape(P, 1))
    rows = [_np.tile(_np.asarray(a).reshape(1, -1), (P, 1)) for a in (L0_conv_dt_b, L0_conv_log_A, L1_attn_bm)]
    laid_out = {
        "x": x,
        "small_params": _np.concatenate(columns + rows, axis=1),
        "attn_weights": _np.stack([_np.asarray(a) for a in (L1_attn_Wh, L1_attn_Wl, L1_attn_Wg, L1_attn_Wm)], axis=1),
        "experts": _np.asarray(L1_ffn_W).transpose(1, 0, 2),
    }

    nc = _bacc.Bacc("TRN2", target_bir_lowering=False, num_devices=1)
    arrays, args = {}, []
    for name, a in laid_out.items():
        a = _np.ascontiguousarray(a)
        arrays[f"in_{name}_dram"] = a
        args.append(nc.dram_tensor(f"in_{name}_dram", a.shape, _mybir.dt.from_np(a.dtype), kind="ExternalInput").ap())
    for i, (shape, dtype) in enumerate(_OUTS):
        dt = _mybir.dt.from_np(_np.dtype(dtype))
        args.append(nc.dram_tensor(f"out_{i}_dram", shape, dt, kind="ExternalOutput").ap())
    conv_attn_hybrid_kernel(nc, *args)
    r = _run(nc, [arrays], core_ids=[0])
    got = tuple(r.results[0][f"out_{i}_dram"] for i in range(len(_OUTS)))
    return got[0]
```

```python
from contextlib import ExitStack

import concourse.bass as bass
from concourse import mybir

ALU = mybir.AluOpType
ACT = mybir.ActivationFunctionType
AX_X = mybir.AxisListType.X
F32 = mybir.dt.float32


def conv_attn_hybrid_kernel(
    nc: bass.Bass,
    x: bass.AP,
    small_params: bass.AP,
    attn_weights: bass.AP,
    W_experts: bass.AP,
    out: bass.AP,
):
    B, C, H, W = x.shape
    P = nc.NUM_PARTITIONS
    N = H * W
    TILES = N // P
    ROWS = P // W
    E = W_experts.shape[1]
    GROUP = C // 32
    BINS = [-1.5, -1.0, -0.5, 0.0, 0.5, 1.0, 1.5]
    EPS = 1e-5
    SOFTPLUS_LINEAR = 40.0
    assert B == 2 and C == P and N % P == 0 and P % W == 0 and E == len(BINS) + 1

    with ExitStack() as ctx:
        def sb(name, shape):
            return ctx.enter_context(nc.sbuf_tensor(name, shape, F32))

        def bank(name):
            return ctx.enter_context(nc.psum_tensor(name, [P, 512], F32))

        def sem(name):
            return ctx.enter_context(nc.semaphore(name))

        identity_sb = sb("identity", [P, P])
        row_mask_sb = sb("row_mask", [P, ROWS])
        identity, row_mask = identity_sb[:, :], row_mask_sb[:, :]
        group_mean = sb("group_mean", [P, P])
        bins = sb("bins", [P, len(BINS)])
        params = sb("params", [P, 3 * TILES + 5 + C])
        ln_col = params[:, 0:2 * TILES]
        bh_col, bl_col, bg_col, dt_w_col, dt_b_col = [params[:, 2 * TILES + i:2 * TILES + i + 1] for i in range(5)]
        log_A_col = params[:, 2 * TILES + 5:3 * TILES + 5]
        bm_row = params[:, 3 * TILES + 5:3 * TILES + 5 + C]
        ln_w_col = [ln_col[:, j:j + 1] for j in range(TILES)]
        ln_b_col = [ln_col[:, TILES + j:TILES + j + 1] for j in range(TILES)]
        ln_dt = sb("ln_dt", [P, 2 * TILES])
        dt_proj = sb("dt_proj", [P, 2 * TILES, ROWS])
        ones = sb("ones", [P, P])
        A = sb("A", [P, TILES])
        neg_A = sb("neg_A", [P, TILES])
        attn_w = sb("attn_w", [P, 4, C])
        wh, wl, wg, wm = [attn_w[:, i, :] for i in range(4)]
        experts = sb("experts", [P, E, C])

        x_sb = sb("x_sb", [P, B, N])
        partial = sb("partial", [P, B, 6])
        moments = sb("moments", [P, B, 3])
        group_moments = sb("group_moments", [P, B, 2])
        var_over_eps = sb("var_over_eps", [P, B])
        mean_sq = sb("mean_sq", [P, B])
        neg_group_var = sb("neg_group_var", [P, B])
        row_var_over_eps = sb("row_var_over_eps", [P, B])
        row_log = sb("row_log", [P, B])
        row_scale = sb("row_scale", [P, B])
        xhat = sb("xhat", [P, B, N])
        xT = sb("xT", [P, B, TILES, C])
        ln_dt_sums = sb("ln_dt_sums", [P, 2, H])
        x_centred = sb("x_centred", [P, B, H])
        dt_bias = sb("dt_bias", [P, H])
        dt = sb("dt", [P, B, H])
        dt_clamped = sb("dt_clamped", [P, B, H])
        dt_exp = sb("dt_exp", [P, B, H])
        dt_log = sb("dt_log", [P, B, H])
        dt_soft = sb("dt_soft", [P, B, N])
        decay = sb("decay", [P, B, TILES, C])
        xn = sb("xn", [P, B, TILES, C])
        scanned = sb("scanned", [P, B, TILES, C])
        tok = sb("tok", [P, B, TILES, C])
        tok_partial = sb("tok_partial", [P, B, TILES, 6])
        tok_moments = sb("tok_moments", [P, B, TILES, 2])
        tok_log = sb("tok_log", [P, B, TILES])
        tok_scale = sb("tok_scale", [P, B, TILES])
        tok_centred = sb("tok_centred", [P, B, C])
        u = sb("u", [P, B, TILES, C])
        uT = sb("uT", [P, B, N])
        hT, lT, gT = sb("hT", [P, B, N]), sb("lT", [P, B, N]), sb("gT", [P, B, N])
        neg_max = sb("neg_max", [P, B, TILES])
        prob_sum = sb("prob_sum", [P, B, TILES])
        prob_scale = sb("prob_scale", [P, B, TILES])
        probs = sb("probs", [P, B, TILES, N])
        probsT = sb("probsT", [P, B, TILES, TILES, P])
        values = sb("values", [P, B, TILES, C])
        skip = sb("skip", [P, B, TILES, C])
        mixed = sb("mixed", [P, B, TILES, C])
        tok2 = sb("tok2", [P, B, TILES, C])
        tok2_partial = sb("tok2_partial", [P, B, TILES, 6])
        tok2_moments = sb("tok2_moments", [P, B, TILES, 2])
        tok2_log = sb("tok2_log", [P, B, TILES])
        tok2_scale = sb("tok2_scale", [P, B, TILES])
        tok2_centred = sb("tok2_centred", [P, B, C])
        v = sb("v", [P, B, TILES, C])
        bin_hits = sb("bin_hits", [P, B, TILES, len(BINS)])
        bin_index = sb("bin_index", [P, B, TILES])
        vT = sb("vT", [P, B, N])
        v_picked = sb("v_picked", [P, B, E, N])
        out_sb = sb("out_sb", [P, B, N])

        warm_operand = nc.const_aps.tensor(1.0, [P, P], mybir.dt.bfloat16)

        banks = [bank(f"bank{i}") for i in range(8)]
        group_ps = banks[0][:, 0:2 * B].rearrange("p (b s) -> p b s", s=2)
        ln_dt_sums_ps = banks[6][:, 0:2 * H].rearrange("p (s r) -> p s r", r=ROWS)
        x_row_ps = banks[3][:, 0:B * H].rearrange("p (b h) -> p b h", b=B)
        xhatT_ps = [[banks[(1, 2, 0, 7)[TILES * b + j]][:, 0:C] for j in range(TILES)] for b in range(B)]
        dtT_ps = [[banks[3][:, 0:C], banks[4][:, 0:C]], [banks[5][:, 0:C], banks[5][:, C:2 * C]]]
        xT_ps = [banks[(5, 7)[b]][:, 0:N].rearrange("p (j c) -> p j c", j=TILES) for b in range(B)]

        def token_tiles(b, n):
            return banks[4 * b + n][:, 0:N].rearrange("p (i c) -> p i c", i=TILES)

        uT_ps = [banks[4 * b][:, 0:N] for b in range(B)]
        hT_ps = [banks[4 * b + 1][:, 0:N] for b in range(B)]
        lT_tile_ps = [banks[2][:, 0:P], banks[6][:, 0:P]]
        lT_last_ps = banks[6][:, 0:N]
        gT_ps = [banks[4 * b + 3][:, 0:N] for b in range(B)]
        scores_ps = [[banks[4 * b + i][:, 0:N] for i in range(TILES)] for b in range(B)]
        skip_ps = [token_tiles(b, 2) for b in range(B)]
        values_ps = [token_tiles(b, 3) for b in range(B)]
        probsT_ps = [[token_tiles(1 - b, 3), token_tiles(b, 3)] for b in range(B)]
        attended_ps = [[banks[4 * b + i][:, 0:C] for i in range(TILES)] for b in range(B)]
        vT_ps = [banks[4 * b][:, 0:N] for b in range(B)]
        bin_ps = [banks[4 * b + 1][:, 0:N] for b in range(B)]
        first_out_ps = banks[2][:, 0:N]
        last_out_ps = [banks[4 * (B - 1) + 2 + i][:, 0:P] for i in range(TILES)]

        def by_batch(name):
            return [sem(f"{name}{b}") for b in range(B)]

        def by_tile(name):
            return [[sem(f"{name}{b}{i}") for i in range(TILES)] for b in range(B)]

        x_loaded = by_batch("x_loaded")
        params_loaded = sem("params_loaded")
        attn_w_loaded = sem("attn_w_loaded")
        experts_loaded = sem("experts_loaded")
        out_stored = sem("out_stored")
        pool_filled = sem("pool_filled")
        identity_ready = sem("identity_ready")
        group_half_cut = sem("group_half_cut")
        group_mean_ready = sem("group_mean_ready")
        mask_half_cut = sem("mask_half_cut")
        row_mask_ready = sem("row_mask_ready")
        bins_ready = sem("bins_ready")
        ln_dt_ready = sem("ln_dt_ready")
        dt_proj_ready = sem("dt_proj_ready")
        xT_turned = by_batch("xT_turned")
        group_summed = sem("group_summed")
        ln_dt_summed = sem("ln_dt_summed")
        x_row_summed = sem("x_row_summed")
        xhat_turned = by_batch("xhat_turned")
        dt_turned = by_batch("dt_turned")
        u_turned = by_batch("u_turned")
        h_projected = by_batch("h_projected")
        l_projected = by_batch("l_projected")
        g_projected = by_batch("g_projected")
        scored = by_batch("scored")
        skip_projected = by_batch("skip_projected")
        values_projected = by_batch("values_projected")
        probs_turned = by_batch("probs_turned")
        attended = by_batch("attended")
        v_turned = by_batch("v_turned")
        bins_spread = by_batch("bins_spread")
        experts_done = by_batch("experts_done")
        ones_ready = sem("ones_ready")
        A_ready = sem("A_ready")
        xT_ready = by_batch("xT_ready")
        partial_ready = by_batch("partial_ready")
        mean_var_ready = by_batch("mean_var_ready")
        moments_ready = by_batch("moments_ready")
        var_over_eps_ready = sem("var_over_eps_ready")
        group_moments_ready = sem("group_moments_ready")
        mean_sq_ready = sem("mean_sq_ready")
        neg_group_var_ready = sem("neg_group_var_ready")
        row_var_ready = sem("row_var_ready")
        row_log_ready = sem("row_log_ready")
        row_scale_ready = sem("row_scale_ready")
        xhat_ready = by_batch("xhat_ready")
        ln_dt_sums_ready = sem("ln_dt_sums_ready")
        dt_bias_ready = sem("dt_bias_ready")
        x_centred_ready = by_batch("x_centred_ready")
        dt_ready = sem("dt_ready")
        dt_clamped_ready = sem("dt_clamped_ready")
        dt_exp_ready = sem("dt_exp_ready")
        dt_log_ready = sem("dt_log_ready")
        dt_soft_ready = by_batch("dt_soft_ready")
        neg_A_ready = sem("neg_A_ready")
        xn_ready = by_tile("xn_ready")
        decay_ready = by_batch("decay_ready")
        scanned_ready = by_batch("scanned_ready")
        tok_ready = by_batch("tok_ready")
        tok_partial_ready = by_batch("tok_partial_ready")
        tok_moments_ready = by_batch("tok_moments_ready")
        tok_log_ready = by_batch("tok_log_ready")
        tok_scale_ready = by_batch("tok_scale_ready")
        tok_centred_ready = by_batch("tok_centred_ready")
        u_ready = by_tile("u_ready")
        uT_ready = by_batch("uT_ready")
        hT_ready = by_batch("hT_ready")
        lT_ready = by_batch("lT_ready")
        gT_ready = by_batch("gT_ready")
        neg_max_ready = by_batch("neg_max_ready")
        probs_ready = by_batch("probs_ready")
        prob_scale_ready = by_batch("prob_scale_ready")
        skip_ready = by_batch("skip_ready")
        values_ready = by_batch("values_ready")
        probsT_ready = by_tile("probsT_ready")
        mixed_ready = by_batch("mixed_ready")
        tok2_ready = by_batch("tok2_ready")
        tok2_partial_ready = by_batch("tok2_partial_ready")
        tok2_moments_ready = by_batch("tok2_moments_ready")
        tok2_log_ready = by_batch("tok2_log_ready")
        tok2_scale_ready = by_batch("tok2_scale_ready")
        tok2_centred_ready = by_batch("tok2_centred_ready")
        v_ready = by_tile("v_ready")
        bin_index_ready = by_batch("bin_index_ready")
        vT_ready = by_batch("vT_ready")
        picked = by_batch("picked")
        out_ready = by_batch("out_ready")
        last_tile_ready = sem("last_tile_ready")

        x_dram = x.rearrange("b c h w -> b c (h w)")
        out_dram = out.rearrange("b c h w -> b c (h w)")

        block = ctx.enter_context(nc.Block())

        @block.sync
        def _(sp):
            for b in range(B):
                sp.dma_start(x_sb[:, b, :], x_dram[b]).then_inc(x_loaded[b], 16)
            sp.dma_start(params[:, :], small_params).then_inc(params_loaded, 16)
            sp.dma_start(attn_w[:, :, :], attn_weights).then_inc(attn_w_loaded, 16)
            sp.dma_start(experts[:, :, :], W_experts).then_inc(experts_loaded, 16)
            sp.wait_ge(out_ready[0], 1)
            sp.dma_start(out_dram[0], out_sb[:, 0, :]).then_inc(out_stored, 16)
            sp.wait_ge(out_ready[1], 1)
            sp.dma_start(out_dram[1][:, 0:P], out_sb[:, 1, 0:P]).then_inc(out_stored, 16)
            sp.wait_ge(out_stored, 16 * 3)

        @block.gpsimd
        def _(pool):
            nc.gpsimd.memset(identity, 0.0).then_inc(pool_filled, 1)
            nc.gpsimd.memset(group_mean[:, :], 1.0 / GROUP).then_inc(pool_filled, 1)
            nc.gpsimd.memset(row_mask, 1.0).then_inc(pool_filled, 1)
            pool.wait_ge(pool_filled, 3)
            nc.gpsimd.affine_select(out=identity, in_=identity, compare_op=ALU.not_equal, fill=1.0,
                                    base=0, pattern=[[-1, P]], channel_multiplier=1).then_inc(identity_ready, 1)
            grouped = group_mean[:, :].rearrange("p (g k) -> p g k", k=GROUP)
            nc.gpsimd.affine_select(out=grouped, in_=grouped, compare_op=ALU.is_ge, fill=0.0, base=0,
                                    pattern=[[-GROUP, P // GROUP], [0, GROUP]],
                                    channel_multiplier=1).then_inc(group_half_cut, 1)
            pool.wait_ge(group_half_cut, 1)
            nc.gpsimd.affine_select(out=grouped, in_=grouped, compare_op=ALU.is_ge, fill=0.0, base=GROUP - 1,
                                    pattern=[[GROUP, P // GROUP], [0, GROUP]],
                                    channel_multiplier=-1).then_inc(group_mean_ready, 1)
            nc.gpsimd.affine_select(out=row_mask, in_=row_mask, compare_op=ALU.is_ge, fill=0.0, base=0,
                                    pattern=[[-W, ROWS]], channel_multiplier=1).then_inc(mask_half_cut, 1)
            pool.wait_ge(mask_half_cut, 1)
            nc.gpsimd.affine_select(out=row_mask, in_=row_mask, compare_op=ALU.is_ge, fill=0.0,
                                    base=W - 1, pattern=[[W, ROWS]],
                                    channel_multiplier=-1).then_inc(row_mask_ready, 1)
            pool.wait_ge(params_loaded, 16)
            nc.gpsimd.tensor_scalar(ln_dt[:, :], ln_col, dt_w_col, None, ALU.mult).then_inc(ln_dt_ready, 1)
            pool.wait_ge(ln_dt_ready, 1)
            nc.gpsimd.tensor_tensor(dt_proj[:, :, :], ln_dt[:, :].unsqueeze(2).to_broadcast([P, 2 * TILES, ROWS]),
                                    row_mask.unsqueeze(1).to_broadcast([P, 2 * TILES, ROWS]),
                                    ALU.mult).then_inc(dt_proj_ready, 1)
            for i, edge in enumerate(BINS):
                nc.gpsimd.memset(bins[:, i:i + 1], edge).then_inc(bins_ready, 1)

        @block.tensor
        def _(pe):
            def stay_warm(scratch, n):
                for _ in range(n):
                    nc.tensor.matmul(scratch[:, 0:P], warm_operand, warm_operand,
                                     start=True, stop=True)

            def turn_x(b):
                pe.wait_ge(x_loaded[b], 16)
                pe.wait_ge(identity_ready, 1)
                for j in range(TILES):
                    last = nc.tensor.transpose(xT_ps[b][:, j, :], x_sb[:, b, j * P:(j + 1) * P], identity)
                last.then_inc(xT_turned[b], 1)

            def sum_groups():
                pe.wait_ge(group_mean_ready, 1)
                for b in range(B):
                    pe.wait_ge(moments_ready[b], 1)
                nc.tensor.matmul(group_ps, group_mean[:, :], moments[:, :, 0:3:2], start=True,
                                 stop=True).then_inc(group_summed, 1)

            def sum_ln_dt():
                pe.wait_ge(ones_ready, 1)
                pe.wait_ge(dt_proj_ready, 1)
                nc.tensor.matmul(ln_dt_sums_ps, ones[:, :], dt_proj[:, :, :], start=True,
                                 stop=True).then_inc(ln_dt_summed, 1)

            def sum_rows(b):
                pe.wait_ge(xT_ready[b], 1)
                for j in range(TILES):
                    nc.tensor.matmul(x_row_ps[:, b, j * ROWS:(j + 1) * ROWS], xT[:, b, j, :], dt_proj[:, j, :],
                                     start=True, stop=True).then_inc(x_row_summed, 1)

            def turn_xhat(b):
                pe.wait_ge(xhat_ready[b], 1)
                if b == 1:
                    pe.wait_ge(group_moments_ready, 1)
                for j in range(TILES):
                    nc.tensor.transpose(xhatT_ps[b][j], xhat[:, b, j * P:(j + 1) * P],
                                        identity).then_inc(xhat_turned[b], 1)

            def turn_dt(b):
                for j in range(TILES):
                    pe.wait_ge(dt_soft_ready[b], j + 1)
                    nc.tensor.transpose(dtT_ps[b][j], dt_soft[:, b, j * P:(j + 1) * P],
                                        identity).then_inc(dt_turned[b], 1)

            def turn_tokens(b):
                for i in range(TILES):
                    pe.wait_ge(u_ready[b][i], 1)
                    last = nc.tensor.transpose(uT_ps[b][:, i * P:(i + 1) * P], u[:, b, i, :], identity)
                last.then_inc(u_turned[b], 1)

            def project_h(b):
                pe.wait_ge(uT_ready[b], 1)
                if b == 0:
                    pe.wait_ge(attn_w_loaded, 16)
                nc.tensor.matmul(hT_ps[b], wh, uT[:, b, :], start=True, stop=True).then_inc(h_projected[b], 1)

            def project_l(b):
                pe.wait_ge(uT_ready[b], 1)
                if b == 0:
                    for i in range(TILES):
                        nc.tensor.matmul(lT_tile_ps[i], wl, uT[:, b, i * P:(i + 1) * P], start=True,
                                         stop=True).then_inc(l_projected[b], 1)
                else:
                    pe.wait_ge(lT_ready[0], TILES)
                    nc.tensor.matmul(lT_last_ps, wl, uT[:, b, :], start=True, stop=True).then_inc(l_projected[b], 1)

            def project_g(b):
                pe.wait_ge(uT_ready[b], 1)
                if b == 1:
                    pe.wait_ge(probsT_ready[0][0], 1)
                nc.tensor.matmul(gT_ps[b], wg, uT[:, b, :], start=True, stop=True).then_inc(g_projected[b], 1)

            def score(b, i):
                pe.wait_ge(hT_ready[b], 1)
                pe.wait_ge(lT_ready[b], i + 1 if b == 0 else 1)
                nc.tensor.matmul(scores_ps[b][i], lT[:, b, i * P:(i + 1) * P], hT[:, b, :],
                                 start=True, stop=True).then_inc(scored[b], 1)

            def project_skip(b):
                pe.wait_ge(lT_ready[b], 1)
                for i in range(TILES):
                    last = nc.tensor.matmul(skip_ps[b][:, i, :], uT[:, b, i * P:(i + 1) * P], wm,
                                            start=True, stop=True)
                last.then_inc(skip_projected[b], 1)

            def project_values(b):
                pe.wait_ge(gT_ready[b], 1)
                for i in range(TILES):
                    last = nc.tensor.matmul(values_ps[b][:, i, :], gT[:, b, i * P:(i + 1) * P], wm,
                                            start=True, stop=True)
                last.then_inc(values_projected[b], 1)

            def turn_probs(b, i):
                pe.wait_ge(probs_ready[b], i + 1)
                if i == 1:
                    pe.wait_ge(values_ready[b], 1)
                elif b == 0:
                    pe.wait_ge(xn_ready[1][1], 1)
                else:
                    pe.wait_ge(probsT_ready[0][1], 1)
                for m in range(TILES):
                    last = nc.tensor.transpose(probsT_ps[b][i][:, m, :], probs[:, b, i, m * P:(m + 1) * P],
                                               identity)
                last.then_inc(probs_turned[b], 1)

            def attend(b, i):
                pe.wait_ge(values_ready[b], 1)
                pe.wait_ge(probsT_ready[b][i], 1)
                for m in range(TILES):
                    last = nc.tensor.matmul(attended_ps[b][i], probsT[:, b, i, m, :], values[:, b, m, :],
                                            start=(m == 0), stop=(m == TILES - 1))
                last.then_inc(attended[b], 1)

            def out_tile(b, i):
                return last_out_ps[i] if b == B - 1 else first_out_ps[:, i * P:(i + 1) * P]

            def carry_residual(b):
                for i in range(TILES):
                    pe.wait_ge(probsT_ready[b][1] if b == B - 1 and i == 1 else skip_ready[b], 1)
                    pe.wait_ge(tok2_ready[b], i + 1)
                    nc.tensor.matmul(out_tile(b, i), tok2[:, b, i, :], identity, is_transpose=True,
                                     start=(b == B - 1 or i == 0), stop=False, skip_group_check=True)

            def turn_v(b):
                for i in range(TILES):
                    pe.wait_ge(v_ready[b][i], 1)
                    last = nc.tensor.transpose(vT_ps[b][:, i * P:(i + 1) * P], v[:, b, i, :], identity)
                last.then_inc(v_turned[b], 1)

            def spread_bins(b):
                for i in range(TILES):
                    pe.wait_ge(bin_index_ready[b], i + 1)
                    last = nc.tensor.transpose(bin_ps[b][:, i * P:(i + 1) * P],
                                               bin_index[:, b, i:i + 1].to_broadcast([P, P]), identity)
                last.then_inc(bins_spread[b], 1)

            def run_expert(b, e):
                if b == 0 and e == 0:
                    pe.wait_ge(experts_loaded, 16)
                pe.wait_ge(picked[b], e + 1)
                if b < B - 1:
                    last = nc.tensor.matmul(first_out_ps, experts[:, e, :], v_picked[:, b, e, :],
                                            start=False, stop=(e == E - 1), skip_group_check=True)
                    if e == E - 1:
                        last.then_inc(experts_done[b], 1)
                else:
                    for i in range(TILES):
                        last = nc.tensor.matmul(last_out_ps[i], experts[:, e, :],
                                                v_picked[:, b, e, i * P:(i + 1) * P],
                                                start=False, stop=(e == E - 1), skip_group_check=True)
                        if e == E - 1:
                            last.then_inc(experts_done[b], 1)

            stay_warm(banks[4], 27)
            turn_x(1)
            turn_x(0)
            sum_groups()
            sum_ln_dt()
            sum_rows(1)
            sum_rows(0)
            stay_warm(banks[4], 26)
            turn_xhat(0)
            turn_dt(0)
            stay_warm(banks[6], 8)
            turn_xhat(1)
            turn_dt(1)
            stay_warm(banks[6], 36)
            turn_tokens(0)
            stay_warm(banks[6], 2)
            project_h(0)
            project_l(0)
            project_g(0)
            turn_tokens(1)
            score(0, 0)
            score(0, 1)
            project_values(0)
            project_skip(0)
            turn_probs(0, 0)
            project_h(1)
            turn_probs(0, 1)
            project_l(1)
            attend(0, 0)
            attend(0, 1)
            project_g(1)
            score(1, 0)
            score(1, 1)
            project_values(1)
            carry_residual(0)
            project_skip(1)
            turn_v(0)
            spread_bins(0)
            turn_probs(1, 0)
            turn_probs(1, 1)
            attend(1, 0)
            attend(1, 1)
            for e in range(0, 3):
                run_expert(0, e)
            carry_residual(1)
            for e in range(3, 6):
                run_expert(0, e)
            turn_v(1)
            spread_bins(1)
            for e in range(6, E):
                run_expert(0, e)
            for e in range(0, E):
                run_expert(1, e)

        @block.vector
        def _(dve):
            nc.vector.memset(ones[:, :], 1.0).then_inc(ones_ready, 1)

            def channel_partial(b):
                dve.wait_ge(x_loaded[b], 16)
                nc.vector.bn_stats(partial[:, b, :], x_sb[:, b, :]).then_inc(partial_ready[b], 1)

            def channel_mean_var(b):
                dve.wait_ge(partial_ready[b], 1)
                nc.vector.bn_aggr(moments[:, b, 0:2], partial[:, b, :]).then_inc(mean_var_ready[b], 1)

            def channel_mean_of_squares(b):
                dve.wait_ge(mean_var_ready[b], 1)
                nc.vector.scalar_tensor_tensor(moments[:, b, 2:3], moments[:, b, 0:1], moments[:, b, 0:1],
                                               moments[:, b, 1:2], ALU.mult, ALU.add).then_inc(moments_ready[b], 1)

            def offset_var():
                for b in range(B):
                    dve.wait_ge(mean_var_ready[b], 1)
                nc.vector.tensor_scalar(var_over_eps[:, :], moments[:, :, 1], 1 / EPS, EPS, ALU.mult,
                                        ALU.add).then_inc(var_over_eps_ready, 1)

            def copy_group_moments():
                dve.wait_ge(group_summed, 1)
                nc.vector.tensor_copy(group_moments[:, :, :], group_ps).then_inc(group_moments_ready, 1)

            def square_group_mean():
                dve.wait_ge(group_moments_ready, 1)
                nc.vector.tensor_tensor(mean_sq[:, :], group_moments[:, :, 0], group_moments[:, :, 0],
                                        ALU.mult).then_inc(mean_sq_ready, 1)

            def negate_group_var():
                dve.wait_ge(mean_sq_ready, 1)
                nc.vector.tensor_tensor(neg_group_var[:, :], mean_sq[:, :], group_moments[:, :, 1],
                                        ALU.subtract).then_inc(neg_group_var_ready, 1)

            def combine_variances():
                dve.wait_ge(neg_group_var_ready, 1)
                dve.wait_ge(var_over_eps_ready, 1)
                nc.vector.scalar_tensor_tensor(row_var_over_eps[:, :], neg_group_var[:, :], 0.0, var_over_eps[:, :],
                                               ALU.min, ALU.subtract, reverse1=True).then_inc(row_var_ready, 1)

            def copy_ln_dt_sums():
                dve.wait_ge(ln_dt_summed, 1)
                nc.vector.tensor_copy(ln_dt_sums[:, :, :].rearrange("p s (j r) -> p (s j) r", r=ROWS),
                                      ln_dt_sums_ps).then_inc(ln_dt_sums_ready, 1)

            def add_dt_bias():
                dve.wait_ge(ln_dt_sums_ready, 1)
                dve.wait_ge(params_loaded, 16)
                nc.vector.tensor_scalar(dt_bias[:, :], ln_dt_sums[:, 1, :], dt_b_col, None,
                                        ALU.add).then_inc(dt_bias_ready, 1)

            def normalize_channels(b):
                dve.wait_ge(row_scale_ready, 1)
                nc.vector.tensor_scalar(xhat[:, b, :], x_sb[:, b, :], moments[:, b, 0:1], row_scale[:, b:b + 1],
                                        ALU.subtract, ALU.mult).then_inc(xhat_ready[b], 1)

            def centre_rows(b):
                dve.wait_ge(x_row_summed, TILES * B)
                dve.wait_ge(ln_dt_sums_ready, 1)
                nc.vector.scalar_tensor_tensor(x_centred[:, b, :], ln_dt_sums[:, 0, :], moments[:, b, 0:1],
                                               x_row_ps[:, b, :], ALU.mult, ALU.subtract,
                                               reverse1=True).then_inc(x_centred_ready[b], 1)

            def project_dt(b):
                dve.wait_ge(dt_bias_ready, 1)
                dve.wait_ge(row_scale_ready, 1)
                dve.wait_ge(x_centred_ready[b], 1)
                nc.vector.scalar_tensor_tensor(dt[:, b, :], x_centred[:, b, :], row_scale[:, b:b + 1], dt_bias[:, :],
                                               ALU.mult, ALU.add).then_inc(dt_ready, 1)

            def clamp_dt():
                dve.wait_ge(dt_ready, B)
                nc.vector.tensor_scalar(dt_clamped[:, :, :], dt[:, :, :], SOFTPLUS_LINEAR, None,
                                        ALU.min).then_inc(dt_clamped_ready, 1)

            def soften_dt(b, j):
                def by_pixel(a):
                    return a[:, b, j * ROWS:(j + 1) * ROWS].unsqueeze(2).to_broadcast([P, ROWS, W])

                dve.wait_ge(dt_log_ready, 1)
                nc.vector.tensor_tensor(dt_soft[:, b, j * P:(j + 1) * P].rearrange("p (r w) -> p r w", w=W),
                                        by_pixel(dt), by_pixel(dt_log), ALU.max).then_inc(dt_soft_ready[b], 1)

            def affine_rows(b, j):
                dve.wait_ge(xhat_turned[b], j + 1)
                dve.wait_ge(params_loaded, 16)
                nc.vector.tensor_scalar(xn[:, b, j, :], xhatT_ps[b][j], ln_w_col[j], ln_b_col[j], ALU.mult,
                                        ALU.add).then_inc(xn_ready[b][j], 1)

            def scan(b, j):
                dve.wait_ge(decay_ready[b], j + 1)
                dve.wait_ge(xn_ready[b][j], 1)
                nc.vector.tensor_tensor_scan(scanned[:, b, j, :], decay[:, b, j, :], xn[:, b, j, :], 0.0,
                                             ALU.mult, ALU.add).then_inc(scanned_ready[b], 1)

            def add_x(b, j):
                dve.wait_ge(xT_ready[b], 1)
                dve.wait_ge(scanned_ready[b], j + 1)
                nc.vector.tensor_tensor(tok[:, b, j, :], scanned[:, b, j, :], xT[:, b, j, :],
                                        ALU.add).then_inc(tok_ready[b], 1)

            def token_partial(b, j):
                dve.wait_ge(tok_ready[b], j + 1)
                nc.vector.bn_stats(tok_partial[:, b, j, :], tok[:, b, j, :]).then_inc(tok_partial_ready[b], 1)

            def token_moments(b, j):
                dve.wait_ge(tok_partial_ready[b], j + 1)
                nc.vector.bn_aggr(tok_moments[:, b, j, :], tok_partial[:, b, j, :]).then_inc(tok_moments_ready[b], 1)

            def centre_tokens(b):
                dve.wait_ge(tok_moments_ready[b], TILES)
                nc.vector.tensor_scalar(tok_centred[:, b, :], tok[:, b, 1, :], tok_moments[:, b, 1, 0:1],
                                        None, ALU.subtract).then_inc(tok_centred_ready[b], 1)

            def normalize_tokens(b, j):
                dve.wait_ge(tok_scale_ready[b], 1)
                nc.vector.tensor_scalar(u[:, b, j, :], tok[:, b, j, :], tok_moments[:, b, j, 0:1],
                                        tok_scale[:, b, j:j + 1], ALU.subtract, ALU.mult).then_inc(u_ready[b][j], 1)

            def relu_l(i):
                dve.wait_ge(l_projected[0], i + 1)
                nc.vector.tensor_scalar(lT[:, 0, i * P:(i + 1) * P], lT_tile_ps[i], bl_col, 0.0, ALU.add,
                                        ALU.max).then_inc(lT_ready[0], 1)

            def relu_g(b):
                dve.wait_ge(g_projected[b], 1)
                nc.vector.tensor_scalar(gT[:, b, :], gT_ps[b], bg_col, 0.0, ALU.add, ALU.max).then_inc(gT_ready[b], 1)

            def score_max(b, i):
                dve.wait_ge(scored[b], i + 1)
                nc.vector.tensor_reduce(neg_max[:, b, i:i + 1], scores_ps[b][i], AX_X, ALU.max,
                                        negate=True).then_inc(neg_max_ready[b], 1)

            def add_skip_bias(b):
                dve.wait_ge(skip_projected[b], 1)
                nc.vector.tensor_tensor(skip[:, b, :, :], skip_ps[b], bm_row.unsqueeze(1).to_broadcast([P, TILES, C]),
                                        ALU.add).then_inc(skip_ready[b], 1)

            def scale_probs(b, i):
                dve.wait_ge(probs_ready[b], i + 1)
                nc.vector.reciprocal(prob_scale[:, b, i:i + 1],
                                     prob_sum[:, b, i:i + 1]).then_inc(prob_scale_ready[b], 1)

            def mix(b, i):
                dve.wait_ge(skip_ready[b], 1)
                dve.wait_ge(attended[b], i + 1)
                dve.wait_ge(prob_scale_ready[b], i + 1)
                nc.vector.scalar_tensor_tensor(mixed[:, b, i, :], attended_ps[b][i], prob_scale[:, b, i:i + 1],
                                               skip[:, b, i, :], ALU.mult, ALU.add).then_inc(mixed_ready[b], 1)

            def add_tokens(b, i):
                dve.wait_ge(mixed_ready[b], i + 1)
                nc.vector.scalar_tensor_tensor(tok2[:, b, i, :], mixed[:, b, i, :], 0.0, tok[:, b, i, :],
                                               ALU.max, ALU.add).then_inc(tok2_ready[b], 1)

            def token2_partial(b, i):
                dve.wait_ge(tok2_ready[b], i + 1)
                nc.vector.bn_stats(tok2_partial[:, b, i, :], tok2[:, b, i, :]).then_inc(tok2_partial_ready[b], 1)

            def token2_moments(b, i):
                dve.wait_ge(tok2_partial_ready[b], i + 1)
                nc.vector.bn_aggr(tok2_moments[:, b, i, :],
                                  tok2_partial[:, b, i, :]).then_inc(tok2_moments_ready[b], 1)

            def centre_tokens2(b):
                dve.wait_ge(tok2_moments_ready[b], TILES)
                nc.vector.tensor_scalar(tok2_centred[:, b, :], tok2[:, b, 1, :], tok2_moments[:, b, 1, 0:1],
                                        None, ALU.subtract).then_inc(tok2_centred_ready[b], 1)

            def normalize_tokens2(b, i):
                dve.wait_ge(tok2_scale_ready[b], 1)
                nc.vector.tensor_scalar(v[:, b, i, :], tok2[:, b, i, :], tok2_moments[:, b, i, 0:1],
                                        tok2_scale[:, b, i:i + 1], ALU.subtract, ALU.mult).then_inc(v_ready[b][i], 1)

            def count_bins(b, i):
                dve.wait_ge(bins_ready, len(BINS))
                dve.wait_ge(v_ready[b][i], 1)
                nc.vector.tensor_scalar(bin_hits[:, b, i, :], bins[:, :], v[:, b, i, 0:1], None, ALU.is_lt,
                                        ALU.add, accum_out=bin_index[:, b, i:i + 1]).then_inc(bin_index_ready[b], 1)

            def pick(b, e):
                dve.wait_ge(bins_spread[b], 1)
                dve.wait_ge(vT_ready[b], 1)
                nc.vector.scalar_tensor_tensor(v_picked[:, b, e, :], bin_ps[b], float(e), vT[:, b, :],
                                               ALU.is_equal, ALU.mult).then_inc(picked[b], 1)

            def copy_out(b):
                dve.wait_ge(experts_done[b], 1)
                if b < B - 1:
                    nc.vector.tensor_copy(out_sb[:, b, :], first_out_ps).then_inc(out_ready[b], 1)
                else:
                    nc.vector.tensor_copy(out_sb[:, b, 0:P], last_out_ps[0]).then_inc(out_ready[b], 1)

            channel_partial(0)
            channel_partial(1)
            channel_mean_var(0)
            channel_mean_var(1)
            channel_mean_of_squares(0)
            channel_mean_of_squares(1)
            copy_group_moments()
            offset_var()
            square_group_mean()
            copy_ln_dt_sums()
            negate_group_var()
            combine_variances()
            add_dt_bias()
            centre_rows(0)
            centre_rows(1)
            project_dt(0)
            project_dt(1)
            clamp_dt()
            normalize_channels(0)
            normalize_channels(1)
            soften_dt(0, 0)
            soften_dt(0, 1)
            affine_rows(0, 0)
            soften_dt(1, 0)
            soften_dt(1, 1)
            scan(0, 0)
            scan(0, 1)
            add_x(0, 0)
            add_x(0, 1)
            token_partial(0, 0)
            token_partial(0, 1)
            token_moments(0, 0)
            token_moments(0, 1)
            scan(1, 0)
            centre_tokens(0)
            scan(1, 1)
            normalize_tokens(0, 0)
            add_x(1, 0)
            add_x(1, 1)
            token_partial(1, 0)
            token_partial(1, 1)
            token_moments(1, 0)
            token_moments(1, 1)
            centre_tokens(1)
            normalize_tokens(1, 0)
            relu_l(0)
            relu_l(1)
            relu_g(0)
            score_max(0, 0)
            score_max(0, 1)
            scale_probs(0, 0)
            add_skip_bias(0)
            scale_probs(0, 1)
            mix(0, 0)
            mix(0, 1)
            add_tokens(0, 0)
            add_tokens(0, 1)
            token2_partial(0, 0)
            token2_partial(0, 1)
            token2_moments(0, 0)
            token2_moments(0, 1)
            score_max(1, 0)
            score_max(1, 1)
            normalize_tokens2(0, 0)
            normalize_tokens2(0, 1)
            count_bins(0, 0)
            scale_probs(1, 0)
            count_bins(0, 1)
            add_skip_bias(1)
            scale_probs(1, 1)
            for e in range(0, 5):
                pick(0, e)
            mix(1, 0)
            mix(1, 1)
            add_tokens(1, 0)
            add_tokens(1, 1)
            token2_partial(1, 0)
            token2_partial(1, 1)
            token2_moments(1, 0)
            token2_moments(1, 1)
            pick(0, 5)
            centre_tokens2(1)
            normalize_tokens2(1, 0)
            pick(0, 6)
            count_bins(1, 0)
            count_bins(1, 1)
            pick(0, 7)
            for e in range(0, 5):
                pick(1, e)
            copy_out(0)
            for e in range(5, E):
                pick(1, e)
            copy_out(1)

        @block.scalar
        def _(act):
            nc.scalar.preload_act_table_set("natural_log_exp_and_others")

            def exponentiate_A():
                act.wait_ge(params_loaded, 16)
                nc.scalar.activation(A[:, :], log_A_col, ACT.Exp).then_inc(A_ready, 1)

            def negate_A():
                act.wait_ge(A_ready, 1)
                nc.scalar.activation(neg_A[:, :], A[:, :], ACT.Copy, scale=-1.0).then_inc(neg_A_ready, 1)

            def copy_xT(b):
                act.wait_ge(xT_turned[b], 1)
                nc.scalar.copy(xT[:, b, :, :], xT_ps[b]).then_inc(xT_ready[b], 1)

            def channel_scale():
                act.wait_ge(row_var_ready, 1)
                nc.scalar.activation(row_log[:, :], row_var_over_eps[:, :], ACT.Ln,
                                     scale=EPS).then_inc(row_log_ready, 1)
                act.wait_ge(row_log_ready, 1)
                nc.scalar.activation(row_scale[:, :], row_log[:, :], ACT.Exp, scale=-0.5).then_inc(row_scale_ready, 1)

            def exponentiate_dt():
                act.wait_ge(dt_clamped_ready, 1)
                nc.scalar.activation(dt_exp[:, :, :], dt_clamped[:, :, :], ACT.Exp).then_inc(dt_exp_ready, 1)

            def log_dt():
                act.wait_ge(dt_exp_ready, 1)
                nc.scalar.activation(dt_log[:, :, :], dt_exp[:, :, :], ACT.Ln, bias=1.0).then_inc(dt_log_ready, 1)

            def affine_rows(b, j):
                act.wait_ge(xhat_turned[b], j + 1)
                act.wait_ge(params_loaded, 16)
                nc.scalar.activation(xn[:, b, j, :], xhatT_ps[b][j], ACT.Identity, bias=ln_b_col[j],
                                     scale=ln_w_col[j]).then_inc(xn_ready[b][j], 1)

            def exponentiate_decay(b, j):
                act.wait_ge(neg_A_ready, 1)
                act.wait_ge(dt_turned[b], j + 1 if b == 0 else TILES)
                nc.scalar.activation(decay[:, b, j, :], dtT_ps[b][j], ACT.Exp,
                                     scale=neg_A[:, j:j + 1]).then_inc(decay_ready[b], 1)

            def token_scale(b):
                act.wait_ge(tok_moments_ready[b], TILES)
                nc.scalar.activation(tok_log[:, b, :], tok_moments[:, b, :, 1], ACT.Ln,
                                     bias=EPS).then_inc(tok_log_ready[b], 1)
                act.wait_ge(tok_log_ready[b], 1)
                nc.scalar.activation(tok_scale[:, b, :], tok_log[:, b, :], ACT.Exp,
                                     scale=-0.5).then_inc(tok_scale_ready[b], 1)

            def scale_tokens(b):
                act.wait_ge(tok_centred_ready[b], 1)
                act.wait_ge(tok_scale_ready[b], 1)
                nc.scalar.activation(u[:, b, 1, :], tok_centred[:, b, :], ACT.Copy,
                                     scale=tok_scale[:, b, 1:2]).then_inc(u_ready[b][1], 1)

            def copy_uT(b):
                act.wait_ge(u_turned[b], 1)
                nc.scalar.copy(uT[:, b, :], uT_ps[b]).then_inc(uT_ready[b], 1)

            def relu_h(b):
                act.wait_ge(h_projected[b], 1)
                nc.scalar.activation(hT[:, b, :], hT_ps[b], ACT.Relu, bias=bh_col).then_inc(hT_ready[b], 1)

            def relu_l_last():
                act.wait_ge(l_projected[1], 1)
                nc.scalar.activation(lT[:, 1, :], lT_last_ps, ACT.Relu, bias=bl_col).then_inc(lT_ready[1], 1)

            def relu_g(b):
                act.wait_ge(g_projected[b], 1)
                nc.scalar.activation(gT[:, b, :], gT_ps[b], ACT.Relu, bias=bg_col).then_inc(gT_ready[b], 1)

            def exponentiate(b, i):
                act.wait_ge(neg_max_ready[b], i + 1)
                nc.scalar.activation(probs[:, b, i, :], scores_ps[b][i], ACT.Exp, bias=neg_max[:, b, i:i + 1],
                                     accum_out=prob_sum[:, b, i:i + 1]).then_inc(probs_ready[b], 1)

            def copy_values(b):
                act.wait_ge(values_projected[b], 1)
                nc.scalar.copy(values[:, b, :, :], values_ps[b]).then_inc(values_ready[b], 1)

            def copy_probsT(b, i):
                act.wait_ge(probs_turned[b], i + 1)
                nc.scalar.copy(probsT[:, b, i, :, :], probsT_ps[b][i]).then_inc(probsT_ready[b][i], 1)

            def token_scale2(b):
                act.wait_ge(tok2_moments_ready[b], TILES)
                nc.scalar.activation(tok2_log[:, b, :], tok2_moments[:, b, :, 1], ACT.Ln,
                                     bias=EPS).then_inc(tok2_log_ready[b], 1)
                act.wait_ge(tok2_log_ready[b], 1)
                nc.scalar.activation(tok2_scale[:, b, :], tok2_log[:, b, :], ACT.Exp,
                                     scale=-0.5).then_inc(tok2_scale_ready[b], 1)

            def scale_tokens2(b):
                act.wait_ge(tok2_centred_ready[b], 1)
                act.wait_ge(tok2_scale_ready[b], 1)
                nc.scalar.activation(v[:, b, 1, :], tok2_centred[:, b, :], ACT.Copy,
                                     scale=tok2_scale[:, b, 1:2]).then_inc(v_ready[b][1], 1)

            def copy_vT(b):
                act.wait_ge(v_turned[b], 1)
                nc.scalar.copy(vT[:, b, :], vT_ps[b]).then_inc(vT_ready[b], 1)

            def copy_out(b):
                if b < B - 1:
                    act.wait_ge(experts_done[b], 1)
                    nc.scalar.copy(out_sb[:, b, :], first_out_ps).then_inc(out_ready[b], 1)
                else:
                    act.wait_ge(experts_done[b], TILES)
                    nc.scalar.copy(out_sb[:, b, P:N], last_out_ps[1]).then_inc(last_tile_ready, 1)
                    act.wait_ge(last_tile_ready, 1)
                    act.dma_start(out_dram[b][:, P:N], out_sb[:, b, P:N]).then_inc(out_stored, 16)

            exponentiate_A()
            copy_xT(0)
            copy_xT(1)
            channel_scale()
            negate_A()
            exponentiate_dt()
            log_dt()
            affine_rows(0, 1)
            exponentiate_decay(0, 0)
            exponentiate_decay(0, 1)
            affine_rows(1, 0)
            exponentiate_decay(1, 0)
            affine_rows(1, 1)
            exponentiate_decay(1, 1)
            token_scale(0)
            scale_tokens(0)
            copy_uT(0)
            token_scale(1)
            scale_tokens(1)
            relu_h(0)
            copy_uT(1)
            exponentiate(0, 0)
            copy_values(0)
            exponentiate(0, 1)
            copy_probsT(0, 0)
            copy_probsT(0, 1)
            relu_l_last()
            relu_h(1)
            relu_g(1)
            token_scale2(0)
            copy_values(1)
            exponentiate(1, 0)
            exponentiate(1, 1)
            copy_vT(0)
            copy_probsT(1, 0)
            copy_probsT(1, 1)
            token_scale2(1)
            scale_tokens2(1)
            copy_vT(1)
            copy_out(1)


_OUTS = [((2, 128, 16, 16), 'float32')]


def kernel(x, L0_conv_log_A, L0_conv_dt_w, L0_conv_dt_b, L0_conv_ln_w, L0_conv_ln_b, L1_attn_Wh, L1_attn_bh,
           L1_attn_Wl, L1_attn_bl, L1_attn_Wg, L1_attn_bg, L1_attn_Wm, L1_attn_bm, L1_ffn_W):
    import numpy as _np
    import concourse.bacc as _bacc
    from concourse import mybir as _mybir
    from concourse.bass_utils import run_bass_kernel_spmd as _run

    P, W = 128, x.shape[3]
    by_partition = [_np.asarray(a).reshape(-1, P).T for a in (
        L0_conv_ln_w, L0_conv_ln_b, L1_attn_bh, L1_attn_bl, L1_attn_bg,
        _np.tile(_np.asarray(L0_conv_dt_w), P // W),
        _np.tile(_np.asarray(L0_conv_dt_b).reshape(1, 1), (P, 1)),
        _np.repeat(_np.asarray(L0_conv_log_A), W))]
    bm_repeated = _np.tile(_np.asarray(L1_attn_bm).reshape(1, -1), (P, 1))
    laid_out = {
        "x": x,
        "small_params": _np.concatenate(by_partition + [bm_repeated], axis=1),
        "attn_weights": _np.stack([_np.asarray(a) for a in (L1_attn_Wh, L1_attn_Wl, L1_attn_Wg, L1_attn_Wm)], axis=1),
        "experts": _np.asarray(L1_ffn_W).transpose(1, 0, 2),
    }

    nc = _bacc.Bacc("TRN2", target_bir_lowering=False, num_devices=1)
    arrays, args = {}, []
    for name, a in laid_out.items():
        a = _np.ascontiguousarray(a)
        arrays[f"in_{name}_dram"] = a
        args.append(nc.dram_tensor(f"in_{name}_dram", a.shape, _mybir.dt.from_np(a.dtype), kind="ExternalInput").ap())
    for i, (shape, dtype) in enumerate(_OUTS):
        dt = _mybir.dt.from_np(_np.dtype(dtype))
        args.append(nc.dram_tensor(f"out_{i}_dram", shape, dt, kind="ExternalOutput").ap())
    conv_attn_hybrid_kernel(nc, *args)
    r = _run(nc, [arrays], core_ids=[0])
    got = tuple(r.results[0][f"out_{i}_dram"] for i in range(len(_OUTS)))
    return got[0]
```
